# Optimizing a Trainium2 kernel written in Bass

```python
import numpy as np
import jax
import jax.numpy as jnp

def _softmax(x, axis=-1):
    return jax.nn.softmax(x, axis=axis)

def _gelu(x):
    return jax.nn.gelu(x, approximate=True)

def _silu(x):
    return jax.nn.silu(x)

def _sigmoid(x):
    return jax.nn.sigmoid(x)

def _layernorm(x, axis=-1, eps=1e-05):
    m = jnp.mean(x, axis=axis, keepdims=True)
    v = jnp.var(x, axis=axis, keepdims=True)
    return (x - m) / jnp.sqrt(v + eps)

def _scatter_add(tgt, idx, src, axis=0):
    return tgt.at[idx].add(src)

def _segment_sum(src, seg, n):
    return jax.ops.segment_sum(src, seg, n)
kernel_name = 'mk_dlrm_tower_d1_rec_r8_b3b5a1'

def setup_inputs(seed: int=0):
    np.random.seed(seed)
    _w = jnp.asarray

    def _rec_inputs():
        import jax
        import jax.numpy as jnp
        _tk = jax.random.key(seed)
        dense_ctx = jax.random.normal(jax.random.fold_in(_tk, 190), (2048, 16), jnp.float32)
        ids = jnp.stack([jax.random.randint(jax.random.fold_in(_tk, 200 + f), (2048,), 0, v, jnp.int32) for f, v in enumerate([1250, 1250, 1000, 1000, 125000, 1000, 12500, 12500, 12500, 12500, 1250, 12500, 12500, 125000, 125000, 125000, 1000, 125000, 125000, 125000, 125000, 125000, 12500, 125000, 12500, 12500, 1000, 1000, 1250, 12500, 1250, 125000])], axis=1)
        tbl_0 = 0.05 * jax.random.normal(jax.random.fold_in(_tk, 500 + 0), (1250, 16), jnp.float32)
        tbl_1 = 0.05 * jax.random.normal(jax.random.fold_in(_tk, 500 + 1), (1250, 16), jnp.float32)
        tbl_2 = 0.05 * jax.random.normal(jax.random.fold_in(_tk, 500 + 2), (1000, 16), jnp.float32)
        tbl_3 = 0.05 * jax.random.normal(jax.random.fold_in(_tk, 500 + 3), (1000, 16), jnp.float32)
        tbl_4 = 0.05 * jax.random.normal(jax.random.fold_in(_tk, 500 + 4), (125000, 16), jnp.float32)
        tbl_5 = 0.05 * jax.random.normal(jax.random.fold_in(_tk, 500 + 5), (1000, 16), jnp.float32)
        tbl_6 = 0.05 * jax.random.normal(jax.random.fold_in(_tk, 500 + 6), (12500, 16), jnp.float32)
        tbl_7 = 0.05 * jax.random.normal(jax.random.fold_in(_tk, 500 + 7), (12500, 16), jnp.float32)
        tbl_8 = 0.05 * jax.random.normal(jax.random.fold_in(_tk, 500 + 8), (12500, 16), jnp.float32)
        tbl_9 = 0.05 * jax.random.normal(jax.random.fold_in(_tk, 500 + 9), (12500, 16), jnp.float32)
        tbl_10 = 0.05 * jax.random.normal(jax.random.fold_in(_tk, 500 + 10), (1250, 16), jnp.float32)
        tbl_11 = 0.05 * jax.random.normal(jax.random.fold_in(_tk, 500 + 11), (12500, 16), jnp.float32)
        tbl_12 = 0.05 * jax.random.normal(jax.random.fold_in(_tk, 500 + 12), (12500, 16), jnp.float32)
        tbl_13 = 0.05 * jax.random.normal(jax.random.fold_in(_tk, 500 + 13), (125000, 16), jnp.float32)
        tbl_14 = 0.05 * jax.random.normal(jax.random.fold_in(_tk, 500 + 14), (125000, 16), jnp.float32)
        tbl_15 = 0.05 * jax.random.normal(jax.random.fold_in(_tk, 500 + 15), (125000, 16), jnp.float32)
        tbl_16 = 0.05 * jax.random.normal(jax.random.fold_in(_tk, 500 + 16), (1000, 16), jnp.float32)
        tbl_17 = 0.05 * jax.random.normal(jax.random.fold_in(_tk, 500 + 17), (125000, 16), jnp.float32)
        tbl_18 = 0.05 * jax.random.normal(jax.random.fold_in(_tk, 500 + 18), (125000, 16), jnp.float32)
        tbl_19 = 0.05 * jax.random.normal(jax.random.fold_in(_tk, 500 + 19), (125000, 16), jnp.float32)
        tbl_20 = 0.05 * jax.random.normal(jax.random.fold_in(_tk, 500 + 20), (125000, 16), jnp.float32)
        tbl_21 = 0.05 * jax.random.normal(jax.random.fold_in(_tk, 500 + 21), (125000, 16), jnp.float32)
        tbl_22 = 0.05 * jax.random.normal(jax.random.fold_in(_tk, 500 + 22), (12500, 16), jnp.float32)
        tbl_23 = 0.05 * jax.random.normal(jax.random.fold_in(_tk, 500 + 23), (125000, 16), jnp.float32)
        tbl_24 = 0.05 * jax.random.normal(jax.random.fold_in(_tk, 500 + 24), (12500, 16), jnp.float32)
        tbl_25 = 0.05 * jax.random.normal(jax.random.fold_in(_tk, 500 + 25), (12500, 16), jnp.float32)
        tbl_26 = 0.05 * jax.random.normal(jax.random.fold_in(_tk, 500 + 26), (1000, 16), jnp.float32)
        tbl_27 = 0.05 * jax.random.normal(jax.random.fold_in(_tk, 500 + 27), (1000, 16), jnp.float32)
        tbl_28 = 0.05 * jax.random.normal(jax.random.fold_in(_tk, 500 + 28), (1250, 16), jnp.float32)
        tbl_29 = 0.05 * jax.random.normal(jax.random.fold_in(_tk, 500 + 29), (12500, 16), jnp.float32)
        tbl_30 = 0.05 * jax.random.normal(jax.random.fold_in(_tk, 500 + 30), (1250, 16), jnp.float32)
        tbl_31 = 0.05 * jax.random.normal(jax.random.fold_in(_tk, 500 + 31), (125000, 16), jnp.float32)
        _rk = jax.random.fold_in(_tk, 7)
        W_top1 = 0.0441942 * jax.random.normal(jax.random.fold_in(_tk, 801), (512, 512), jnp.float32)
        W_top2 = 0.0441942 * jax.random.normal(jax.random.fold_in(_tk, 802), (512, 256), jnp.float32)
        W_top3 = 0.0625 * jax.random.normal(jax.random.fold_in(_tk, 803), (256, 1), jnp.float32)
        b_top1 = jnp.zeros((512,), jnp.float32)
        b_top2 = jnp.zeros((256,), jnp.float32)
        return (dense_ctx, ids, tbl_0, tbl_1, tbl_2, tbl_3, tbl_4, tbl_5, tbl_6, tbl_7, tbl_8, tbl_9, tbl_10, tbl_11, tbl_12, tbl_13, tbl_14, tbl_15, tbl_16, tbl_17, tbl_18, tbl_19, tbl_20, tbl_21, tbl_22, tbl_23, tbl_24, tbl_25, tbl_26, tbl_27, tbl_28, tbl_29, tbl_30, tbl_31, W_top1, b_top1, W_top2, b_top2, W_top3)
    dense_ctx, ids, tbl_0, tbl_1, tbl_2, tbl_3, tbl_4, tbl_5, tbl_6, tbl_7, tbl_8, tbl_9, tbl_10, tbl_11, tbl_12, tbl_13, tbl_14, tbl_15, tbl_16, tbl_17, tbl_18, tbl_19, tbl_20, tbl_21, tbl_22, tbl_23, tbl_24, tbl_25, tbl_26, tbl_27, tbl_28, tbl_29, tbl_30, tbl_31, W_top1, b_top1, W_top2, b_top2, W_top3 = _rec_inputs()

    def _L0_rec_setup():
        import jax, jax.numpy as jnp
        import numpy as np

        def _pair_indices(num_fields: int):
            row, col = ([], [])
            for i in range(num_fields - 1):
                for j in range(i + 1, num_fields):
                    row.append(i)
                    col.append(j)
            return (np.asarray(row, dtype=np.int32), np.asarray(col, dtype=np.int32))
        key = jax.random.key(seed)
        B, F, D = (2048, 32, 16)
        x = jax.random.normal(key, (B, F, D), dtype=jnp.float32)
        return {'x': x}
    _L0_rec_all = _L0_rec_setup()
    _L0_rec_in = {k: v for k, v in _L0_rec_all.items() if k in ()}
    del _L0_rec_all
    return {'dense_ctx': dense_ctx, 'ids': ids, 'tbl_0': tbl_0, 'tbl_1': tbl_1, 'tbl_2': tbl_2, 'tbl_3': tbl_3, 'tbl_4': tbl_4, 'tbl_5': tbl_5, 'tbl_6': tbl_6, 'tbl_7': tbl_7, 'tbl_8': tbl_8, 'tbl_9': tbl_9, 'tbl_10': tbl_10, 'tbl_11': tbl_11, 'tbl_12': tbl_12, 'tbl_13': tbl_13, 'tbl_14': tbl_14, 'tbl_15': tbl_15, 'tbl_16': tbl_16, 'tbl_17': tbl_17, 'tbl_18': tbl_18, 'tbl_19': tbl_19, 'tbl_20': tbl_20, 'tbl_21': tbl_21, 'tbl_22': tbl_22, 'tbl_23': tbl_23, 'tbl_24': tbl_24, 'tbl_25': tbl_25, 'tbl_26': tbl_26, 'tbl_27': tbl_27, 'tbl_28': tbl_28, 'tbl_29': tbl_29, 'tbl_30': tbl_30, 'tbl_31': tbl_31, 'W_top1': W_top1, 'b_top1': b_top1, 'W_top2': W_top2, 'b_top2': b_top2, 'W_top3': W_top3}

def reference(dense_ctx, ids, tbl_0, tbl_1, tbl_2, tbl_3, tbl_4, tbl_5, tbl_6, tbl_7, tbl_8, tbl_9, tbl_10, tbl_11, tbl_12, tbl_13, tbl_14, tbl_15, tbl_16, tbl_17, tbl_18, tbl_19, tbl_20, tbl_21, tbl_22, tbl_23, tbl_24, tbl_25, tbl_26, tbl_27, tbl_28, tbl_29, tbl_30, tbl_31, W_top1, b_top1, W_top2, b_top2, W_top3):
    import jax
    import jax.numpy as jnp

    def _L0_rec_ref(x):
        import jax, jax.numpy as jnp
        import numpy as np

        def _pair_indices(num_fields: int):
            row, col = ([], [])
            for i in range(num_fields - 1):
                for j in range(i + 1, num_fields):
                    row.append(i)
                    col.append(j)
            return (np.asarray(row, dtype=np.int32), np.asarray(col, dtype=np.int32))
        num_fields = x.shape[1]
        row, col = _pair_indices(num_fields)
        return jnp.sum(x[:, row, :] * x[:, col, :], axis=2)
    e = jnp.stack([tbl_0[ids[:, 0]], tbl_1[ids[:, 1]], tbl_2[ids[:, 2]], tbl_3[ids[:, 3]], tbl_4[ids[:, 4]], tbl_5[ids[:, 5]], tbl_6[ids[:, 6]], tbl_7[ids[:, 7]], tbl_8[ids[:, 8]], tbl_9[ids[:, 9]], tbl_10[ids[:, 10]], tbl_11[ids[:, 11]], tbl_12[ids[:, 12]], tbl_13[ids[:, 13]], tbl_14[ids[:, 14]], tbl_15[ids[:, 15]], tbl_16[ids[:, 16]], tbl_17[ids[:, 17]], tbl_18[ids[:, 18]], tbl_19[ids[:, 19]], tbl_20[ids[:, 20]], tbl_21[ids[:, 21]], tbl_22[ids[:, 22]], tbl_23[ids[:, 23]], tbl_24[ids[:, 24]], tbl_25[ids[:, 25]], tbl_26[ids[:, 26]], tbl_27[ids[:, 27]], tbl_28[ids[:, 28]], tbl_29[ids[:, 29]], tbl_30[ids[:, 30]], tbl_31[ids[:, 31]]], axis=1)
    z = _L0_rec_ref(e)
    z = z.reshape(z.shape[0], -1)
    h = jnp.concatenate([z, dense_ctx], axis=1)
    h = jnp.maximum(h @ W_top1 + b_top1, 0.0)
    h = jnp.maximum(h @ W_top2 + b_top2, 0.0)
    y = h @ W_top3
    return y

_drawn_inputs = setup_inputs


def setup_inputs(seed=0):
    import zlib

    import numpy as np

    out = dict(_drawn_inputs(seed))
    spreads = {'b_top1': (0.0, 0.1), 'b_top2': (0.0, 0.1)}
    factors = {'tbl_0': 5.231,
     'tbl_1': 4.955,
     'tbl_2': 4.657,
     'tbl_3': 4.567,
     'tbl_4': 3.919,
     'tbl_5': 5.076,
     'tbl_6': 4.515,
     'tbl_7': 3.934,
     'tbl_8': 4.548,
     'tbl_9': 4.375,
     'tbl_10': 4.583,
     'tbl_11': 4.352,
     'tbl_12': 4.219,
     'tbl_13': 4.098,
     'tbl_14': 4.627,
     'tbl_15': 4.488,
     'tbl_16': 4.164,
     'tbl_17': 4.649,
     'tbl_18': 4.185,
     'tbl_19': 4.37,
     'tbl_20': 4.261,
     'tbl_21': 4.431,
     'tbl_22': 4.8,
     'tbl_23': 4.751,
     'tbl_24': 4.582,
     'tbl_25': 4.172,
     'tbl_26': 4.625,
     'tbl_27': 4.447,
     'tbl_28': 4.845,
     'tbl_29': 4.582,
     'tbl_30': 4.493,
     'tbl_31': 4.807}
    for name, (base, spread) in spreads.items():
        noise = np.random.default_rng([zlib.crc32(name.encode()), seed]).standard_normal(out[name].shape)
        drawn = base * np.exp(spread * noise) if base else spread * noise
        out[name] = jnp.asarray(drawn.astype(out[name].dtype))
    for name, factor in factors.items():
        out[name] = (out[name] * factor).astype(out[name].dtype)
    return out
```

```python
from collections import namedtuple
from contextlib import ExitStack

import concourse.bass as bass
from concourse import mybir

P = 128
TILES = 2
SLOTS = 2 * TILES
PRODS = 2
ROUND = float(3 * 2 ** 22)

F32 = mybir.dt.float32
BF16 = mybir.dt.bfloat16
F16 = mybir.dt.float16
I32 = mybir.dt.int32
ALU = mybir.AluOpType
ACT = mybir.ActivationFunctionType
AX_X = mybir.AxisListType.X

Kind = namedtuple("Kind", "name fields first rows outer inner number")


def pair_blocks(fields):
    blocks, at, half = [], 0, fields // 2
    while half:
        blocks.append((half, at))
        at += (fields // (2 * half)) * half * half
        half //= 2
    return blocks, at


def free(turn, signals=1):
    return signals * (turn + 1)


def done(turn, signals=1, buffers=1):
    return signals * (turn + 1 + buffers)


def dlrm_tower(nc, kinds, dense, ids, ids_by_half, looked_tables, gathered_tables, consts, w1, b1, w2, b2, w3,
               identity, out):
    B, F = ids.shape
    D = gathered_tables[0].shape[1]
    TERMS = D // 2
    KINDS = len(kinds)
    LOOKED = sum(k.fields for k in kinds)
    GATHERED = F - LOOKED
    N1, N2 = w1.shape[1], w2.shape[1]
    ND = dense.shape[1]
    HALF = P * TILES
    HALVES = B // HALF
    GROUPS = B // (P * SLOTS)
    K1, K2, K3 = w1.shape[0] // P, N1 // P, N2 // P
    blocks, PAIRS = pair_blocks(F)
    STEPS = sum(k.outer for k in kinds)
    IOTA = consts.shape[1] - max(k.inner for k in kinds)
    assert PAIRS + ND == w1.shape[0] and STEPS % 2 == 0

    with ExitStack() as ctx:
        def sb(name, shape, dt=F32):
            return ctx.enter_context(nc.sbuf_tensor(name, shape, dt))

        def psum(name, shape):
            return ctx.enter_context(nc.psum_tensor(name, shape, F32))

        def sem(name):
            return ctx.enter_context(nc.semaphore(name))

        def sems(name, n):
            return [sem(f"{name}{i}") for i in range(n)]

        idx = sb("idx", [P, SLOTS, GATHERED], I32)
        idx_looked = sb("idx_looked", [P, B // P, LOOKED], I32)
        emb = sb("emb", [P, SLOTS, F * D])
        dense_sb = sb("dense_sb", [P, B // P, ND])
        prod = sb("prod", [P, PRODS, D, PAIRS + ND])
        zT = sb("zT", [P, K1, HALF])
        h1 = sb("h1", [P, K2, HALF])
        h2 = sb("h2", [P, K3, HALF])
        y = sb("y", [1, B])
        w1_sb = sb("w1_sb", [P, K1, N1])
        w2_sb = sb("w2_sb", [P, K2, N2])
        w3_sb = sb("w3_sb", [P, K3])
        b1_sb = sb("b1_sb", [P, K2])
        b2_sb = sb("b2_sb", [P, K3])
        ident = sb("ident", [P, P])
        const = sb("const", [P, consts.shape[1]])
        rows_in = sb("rows_in", [HALVES * LOOKED, HALF], I32)
        scaled_rows = sb("scaled_rows", [HALVES * LOOKED, HALF])
        numbers = sb("numbers", [HALVES * LOOKED, HALF], F16)
        numbers_dram = nc.dram_tensor("numbers_dram", (HALVES * LOOKED, HALF), F16, kind="Internal").ap()
        wide = sb("wide", [P, LOOKED, HALF], F16)
        dist = sb("dist", [P, 2, max(k.fields for k in kinds), HALF], BF16)
        hot = [sb(f"hot_{k.name}", [P, 2, k.outer, k.fields, HALF], BF16) for k in kinds]
        parts = [sb(f"parts_{k.name}", [P, k.fields * k.outer, 3, k.inner * D], BF16) for k in kinds]
        mask = [sb(f"mask_{k.name}", [P, B // P, k.fields, k.inner]) for k in kinds]
        picked = [sb(f"picked_{k.name}", [P, k.fields * k.inner, D]) for k in kinds]
        block_of = sb("block_of", [P, B // P, LOOKED])
        within = sb("within", [P, B // P, LOOKED])
        prod_flat = prod[:, :, :, :].rearrange("p b d q -> p (b d q)")
        raw, at = [], 0
        for k in kinds:
            size = k.fields * k.outer * k.inner * D
            raw.append(prod_flat[0:k.rows, at:at + size].rearrange("p (a c) -> p a c", c=k.inner * D))
            at += size

        zT_ps = [psum(f"zT_ps{i}", [P, K1, P]) for i in range(2)]
        mlp_ps = [psum(f"mlp_ps{i}", [P, 512]) for i in range(2)]
        y_ps = psum("y_ps", [1, HALF])
        rows_ps = [psum(f"rows_ps_{k.name}", [P, k.fields * k.inner * D]) for k in kinds]

        weights_loaded = sem("weights_loaded")
        const_loaded = sem("const_loaded")
        ids_loaded = sem("ids_loaded")
        tables_loaded = sems("tables_loaded", KINDS)
        high_made = sem("high_made")
        rest_made = sem("rest_made")
        middle_made = sem("middle_made")
        low_made = sem("low_made")
        blocks_found = sem("blocks_found")
        within_found = sem("within_found")
        masks_made = sem("masks_made")
        rows_in_loaded = sem("rows_in_loaded")
        rows_scaled = sem("rows_scaled")
        numbers_made = sem("numbers_made")
        numbers_stored = sem("numbers_stored")
        wide_loaded = sem("wide_loaded")
        dist_made = sem("dist_made")
        hot_made = sem("hot_made")
        looked_up = sems("looked_up", KINDS)
        masked = sems("masked", KINDS)
        selected = sem("selected")
        idx_loaded = sems("idx_loaded", SLOTS)
        dense_loaded = sem("dense_loaded")
        gather_begun = sem("gather_begun")
        gathered = sems("gathered", SLOTS)
        multiplied = sems("multiplied", SLOTS)
        halved = sem("halved")
        summed = sem("summed")
        zT_copied = sem("zT_copied")
        h1_made = sem("h1_made")
        h1_relu = sem("h1_relu")
        h2_made = sem("h2_made")
        h2_relu = sem("h2_relu")
        y_made = sem("y_made")
        y_copied = sem("y_copied")
        y_stored = sem("y_stored")

        block = ctx.enter_context(nc.Block())

        @block.sync
        def _(sp):
            def load_idx(s, row):
                sp.dma_start(idx[:, s, :], ids[bass.ds(row, P), LOOKED:]).then_inc(idx_loaded[s], 16)

            for s in range(SLOTS):
                load_idx(s, s * P)
            sp.dma_start(rows_in[:, :], ids_by_half).then_inc(rows_in_loaded, 16)
            sp.dma_start(const[:, :], consts).then_inc(const_loaded, 16)
            for n, k in enumerate(kinds):
                for i, table in enumerate(looked_tables[n]):
                    sp.dma_start(raw[n][:, i * k.outer:(i + 1) * k.outer, :],
                                 table.rearrange("(p a c) d -> p a (c d)", p=k.rows, a=k.outer)
                                 ).then_inc(tables_loaded[n], 16)
            sp.dma_start(idx_looked[:, :, :], ids.rearrange("(t p) f -> p t f", p=P)[:, :, 0:LOOKED]
                         ).then_inc(ids_loaded, 16)
            sp.dma_start(dense_sb[:, :, :], dense.rearrange("(t p) n -> p t n", p=P)).then_inc(dense_loaded, 16)
            with sp.Fori(1, GROUPS) as g:
                for s in range(SLOTS):
                    sp.wait_ge(gathered[s], 16 * GATHERED * g)
                    load_idx(s, (g * SLOTS + s) * P)

        @block.gpsimd
        def _(pool):
            with pool.Fori(0, GROUPS) as g:
                for s in range(SLOTS):
                    pool.wait_ge(multiplied[s], free(g))
                    pool.wait_ge(idx_loaded[s], 16 * (g + 1))
                    pool.sem_inc(gather_begun, 1)
                    for i in range(GATHERED):
                        f = LOOKED + i
                        nc.gpsimd.indirect_dma_start(
                            emb[:, s, f * D:(f + 1) * D], None, gathered_tables[i],
                            bass.IndirectOffsetOnAxis(ap=idx[:, s, i:i + 1], axis=0)).then_inc(gathered[s], 16)

        @block.scalar
        def _(act):
            def load_wide(half):
                act.wait_ge(hot_made, 2 + STEPS * half)
                numbers_by_half = numbers_dram.rearrange("(h f) n -> h (f n)", f=LOOKED)
                act.dma_start(wide[:, :, :].rearrange("p f n -> p (f n)"),
                              numbers_by_half[bass.ds(half, 1), :].to_broadcast([P, LOOKED * HALF])
                              ).then_inc(wide_loaded, 16)

            def one_hot(q, half, n, begin, end):
                k = kinds[n]
                step = sum(j.outer for j in kinds[:n])

                def distance(a):
                    act.wait_ge(hot_made, STEPS * half + free(step + a))
                    nc.scalar.activation(dist[0:k.rows, (step + a) % 2, 0:k.fields, :],
                                         wide[0:k.rows, k.first:k.first + k.fields, :], ACT.Abs,
                                         bias=const[0:k.rows, k.number + a:k.number + a + 1]).then_inc(dist_made, 1)

                act.wait_ge(wide_loaded, 16 * (half + 1))
                act.wait_ge(looked_up[n], free(half, TILES))
                distance(begin)
                for a in range(begin, end):
                    if a + 1 < end:
                        distance(a + 1)
                    act.wait_ge(dist_made, STEPS * half + step + a + 1)
                    nc.scalar.activation(hot[n][0:k.rows, q, a, :, :], dist[0:k.rows, (step + a) % 2, 0:k.fields, :],
                                         ACT.Relu, bias=const[0:k.rows, 0:1], scale=-1.0).then_inc(hot_made, 1)

            def half_work(g, q, ahead):
                half = 2 * g + q
                last = KINDS - 1
                outer = kinds[last].outer
                if ahead:
                    load_wide(half + 2)
                act.wait_ge(h1_made, free(half, K2))
                for i in range(TILES):
                    s = q * TILES + i
                    act.wait_ge(summed, done(g * SLOTS + s, 1, PRODS))
                    nc.scalar.copy(zT[:, :, i * P:(i + 1) * P], zT_ps[s % 2][:, :, :]).then_inc(zT_copied, 1)
                    if ahead and i == 0:
                        for n in range(last):
                            one_hot(q, half + 2, n, 0, kinds[n].outer)
                        one_hot(q, half + 2, last, 0, outer // 2)
                act.wait_ge(h2_made, free(half, K3))
                for m in range(K2):
                    act.wait_ge(h1_made, free(half, K2) + m + 1)
                    nc.scalar.activation(h1[:, m, :], mlp_ps[m % 2][:, 0:HALF], ACT.Relu,
                                         bias=b1_sb[:, m:m + 1]).then_inc(h1_relu, 1)
                act.wait_ge(y_made, free(half))
                for m in range(K3):
                    act.wait_ge(h2_made, free(half, K3) + m + 1)
                    nc.scalar.activation(h2[:, m, :], mlp_ps[m % 2][:, 0:HALF], ACT.Relu,
                                         bias=b2_sb[:, m:m + 1]).then_inc(h2_relu, 1)
                act.wait_ge(y_made, done(half))
                nc.scalar.copy(y[:, bass.ds(half * HALF, HALF)], y_ps[0:1, :]).then_inc(y_copied, 1)
                act.wait_ge(y_copied, done(half))
                act.dma_start(out[bass.ds(half * HALF, HALF), :].rearrange("b o -> o b"),
                              y[:, bass.ds(half * HALF, HALF)]).then_inc(y_stored, 16)
                if ahead:
                    one_hot(q, half + 2, last, outer // 2, outer)

            for signal, count in ((hot_made, 2), (zT_copied, 2), (h1_relu, K2), (h2_relu, K3), (y_copied, 1)):
                act.sem_inc(signal, count)
            for tensor, source in ((ident[:, :], identity), (b1_sb[:, :], b1), (b2_sb[:, :], b2), (w3_sb[:, :], w3),
                                   (w1_sb[:, :, :], w1.rearrange("(c p) n -> p c n", p=P)),
                                   (w2_sb[:, :, :], w2.rearrange("(c p) n -> p c n", p=P))):
                act.dma_start(tensor, source).then_inc(weights_loaded, 16)
            act.wait_ge(numbers_made, 1)
            act.dma_start(numbers_dram, numbers[:, :]).then_inc(numbers_stored, 16)
            act.wait_ge(numbers_stored, 16)
            load_wide(0)
            act.wait_ge(const_loaded, 16)
            for n, k in enumerate(kinds):
                act.wait_ge(tables_loaded[n], 16 * k.fields)
                nc.scalar.copy(parts[n][0:k.rows, :, 0, :], raw[n]).then_inc(high_made, 1)
            for n, k in enumerate(kinds):
                act.wait_ge(rest_made, n + 1)
                nc.scalar.copy(parts[n][0:k.rows, :, 1, :], raw[n]).then_inc(middle_made, 1)
            for n, k in enumerate(kinds):
                one_hot(0, 0, n, 0, k.outer)
            load_wide(1)
            for n, k in enumerate(kinds):
                one_hot(1, 1, n, 0, k.outer)
            act.wait_ge(weights_loaded, 16 * 6)
            with act.Fori(0, GROUPS - 1) as g:
                half_work(g, 0, True)
                half_work(g, 1, True)
            half_work(GROUPS - 1, 0, False)
            half_work(GROUPS - 1, 1, False)
            act.wait_ge(y_stored, 16 * 2 * GROUPS)

        @block.vector
        def _(dve):
            def make_masks():
                for k in kinds:
                    f = slice(k.first, k.first + k.fields)
                    nc.vector.tensor_scalar(within[:, :, f], idx_looked[:, :, f], -(k.inner - 1) / 2, 1.0 / k.inner,
                                            ALU.add, ALU.mult).then_inc(blocks_found, 1)
                dve.wait_ge(blocks_found, KINDS)
                nc.vector.tensor_scalar(block_of[:, :, :], within[:, :, :], ROUND, ROUND,
                                        ALU.add, ALU.subtract).then_inc(blocks_found, 1)
                dve.wait_ge(blocks_found, KINDS + 1)
                for k in kinds:
                    f = slice(k.first, k.first + k.fields)
                    nc.vector.scalar_tensor_tensor(within[:, :, f], block_of[:, :, f], -float(k.inner),
                                                   idx_looked[:, :, f], ALU.mult, ALU.add).then_inc(within_found, 1)
                dve.wait_ge(within_found, KINDS)
                for n, k in enumerate(kinds):
                    shape = [P, B // P, k.fields, k.inner]
                    nc.vector.tensor_tensor(
                        mask[n][:, :, :, :],
                        within[:, :, k.first:k.first + k.fields].unsqueeze(3).to_broadcast(shape),
                        const[:, IOTA:IOTA + k.inner].unsqueeze(1).unsqueeze(1).to_broadcast(shape),
                        ALU.is_equal).then_inc(masks_made, 1)

            def number_blocks():
                c = const[0:HALVES * LOOKED, :]
                nc.vector.tensor_scalar(scaled_rows[:, :], rows_in[:, :], c[:, 1:2], c[:, 2:3],
                                        ALU.mult, ALU.add).then_inc(rows_scaled, 1)
                dve.wait_ge(rows_scaled, 1)
                nc.vector.tensor_scalar(numbers[:, :], scaled_rows[:, :], ROUND, ROUND,
                                        ALU.add, ALU.subtract).then_inc(numbers_made, 1)

            def split_tables():
                for n, k in enumerate(kinds):
                    dve.wait_ge(high_made, n + 1)
                    nc.vector.tensor_tensor(raw[n], raw[n], parts[n][0:k.rows, :, 0, :],
                                            ALU.subtract).then_inc(rest_made, 1)
                for n, k in enumerate(kinds):
                    dve.wait_ge(middle_made, n + 1)
                    nc.vector.tensor_tensor(parts[n][0:k.rows, :, 2, :], raw[n], parts[n][0:k.rows, :, 1, :],
                                            ALU.subtract).then_inc(low_made, 1)

            def select(g, s):
                tile = g * SLOTS + s
                for n, k in enumerate(kinds):
                    dve.wait_ge(looked_up[n], done(tile, 1, SLOTS))
                    dve.wait_ge(selected, KINDS * tile + n + 1)
                    at_tile = mask[n][:, bass.ds(tile, 1), :, :].rearrange("p t f a -> p (t f a)")
                    nc.vector.tensor_tensor(
                        picked[n][:, :, :], rows_ps[n][:, :].rearrange("p (a d) -> p a d", d=D),
                        at_tile.unsqueeze(2).to_broadcast([P, k.fields * k.inner, D]),
                        ALU.mult).then_inc(masked[n], 1)
                dve.wait_ge(multiplied[s], free(g))
                for n, k in enumerate(kinds):
                    dve.wait_ge(masked[n], done(tile))
                    nc.vector.reduce_sum(
                        emb[:, s, k.first * D:(k.first + k.fields) * D].rearrange("p (f d) -> p f d", d=D),
                        picked[n][:, :, :].rearrange("p (f a) d -> p f d a", a=k.inner),
                        AX_X).then_inc(selected, 1)

            def multiply(s, half, at):
                n = F // (2 * half)
                e = emb[:, s, :].rearrange("p (b u j d) -> p b u j d", b=n, u=2, j=half)
                o = prod[:, s % PRODS, :, at:at + n * half * half].rearrange(
                    "p d (b j i) -> p b j i d", b=n, j=half, i=half)
                if n < half:
                    for b in range(n):
                        low = e[:, b, 0, :, :].unsqueeze(1).to_broadcast([P, half, half, D])
                        high = e[:, b, 1, :, :].unsqueeze(2).to_broadcast([P, half, half, D])
                        last = nc.vector.tensor_tensor(o[:, b, :, :, :], low, high, ALU.mult)
                else:
                    for j in range(half):
                        high = e[:, :, 1, j, :].unsqueeze(2).to_broadcast([P, n, half, D])
                        last = nc.vector.tensor_tensor(o[:, :, j, :, :], e[:, :, 0, :, :], high, ALU.mult)
                return last

            def pairs(g, s):
                tile = g * SLOTS + s
                dve.wait_ge(summed, free(tile))
                at_tile = dense_sb[:, bass.ds(tile, 1), :].rearrange("p t n -> p (t n)")
                nc.vector.tensor_copy(prod[:, s % PRODS, 0, PAIRS:], at_tile)
                dve.wait_ge(selected, done(tile, KINDS))
                dve.wait_ge(gathered[s], 16 * GATHERED * (g + 1))
                for half, at in blocks:
                    last = multiply(s, half, at)
                last.then_inc(multiplied[s], 1)
                dve.wait_ge(multiplied[s], done(g))
                terms = prod[:, s % PRODS, :, 0:PAIRS]
                nc.vector.tensor_tensor(terms[:, 0:TERMS, :], terms[:, 0:TERMS, :], terms[:, TERMS:, :],
                                        ALU.add).then_inc(halved, 1)

            for signal, count in ((selected, KINDS), *((m, 1) for m in (*masked, *multiplied))):
                dve.sem_inc(signal, count)
            dve.wait_ge(const_loaded, 16)
            dve.wait_ge(rows_in_loaded, 16)
            number_blocks()
            dve.wait_ge(ids_loaded, 16)
            make_masks()
            split_tables()
            dve.wait_ge(dense_loaded, 16)
            dve.wait_ge(masks_made, KINDS)
            dve.wait_ge(low_made, KINDS)
            select(0, 0)
            with dve.Fori(0, GROUPS - 1) as g:
                for s in range(SLOTS):
                    pairs(g, s)
                    select(g + (s + 1) // SLOTS, (s + 1) % SLOTS)
            for s in range(SLOTS):
                pairs(GROUPS - 1, s)
                if s + 1 < SLOTS:
                    select(GROUPS - 1, s + 1)

        @block.tensor
        def _(pe):
            def look_up(g, s):
                tile = g * SLOTS + s
                half = 2 * g + s // TILES
                cols = slice((s % TILES) * P, (s % TILES + 1) * P)
                steps = 0
                for n, k in enumerate(kinds):
                    steps += k.outer
                    pe.wait_ge(hot_made, 2 + STEPS * half + steps)
                    pe.wait_ge(masked[n], free(tile))
                    for f in range(k.fields):
                        for a in range(k.outer):
                            for part in range(3):
                                last = nc.tensor.matmul(
                                    rows_ps[n][:, f * k.inner * D:(f + 1) * k.inner * D],
                                    hot[n][0:k.rows, s // TILES, a, f, cols],
                                    parts[n][0:k.rows, f * k.outer + a, part, :],
                                    start=(a == 0 and part == 0), stop=(a == k.outer - 1 and part == 2))
                    last.then_inc(looked_up[n], 1)

            def sum_pairs(g, s):
                tile = g * SLOTS + s
                pe.wait_ge(halved, tile + 1)
                pe.wait_ge(zT_copied, free(tile))
                for c in range(K1):
                    for d in range(TERMS):
                        n = P if d == 0 else min(P, PAIRS - c * P)
                        last = nc.tensor.matmul(
                            zT_ps[s % 2][0:n, c, :], prod[:, s % PRODS, d, c * P:c * P + n], ident[:, :],
                            start=(d == 0), stop=(d == TERMS - 1), is_transpose=True)
                last.then_inc(summed, 1)

            def layers(half):
                pe.wait_ge(zT_copied, done(TILES * half + TILES - 1, 1, 2))
                for m in range(K2):
                    if m >= 2:
                        pe.wait_ge(h1_relu, free(half, K2) + m - 1)
                    else:
                        pe.wait_ge(h2_relu, free(half, K3))
                    for c in range(K1):
                        last = nc.tensor.matmul(mlp_ps[m % 2][:, 0:HALF], w1_sb[:, c, m * P:(m + 1) * P], zT[:, c, :],
                                                start=(c == 0), stop=(c == K1 - 1))
                    last.then_inc(h1_made, 1)
                for m in range(K3):
                    pe.wait_ge(h1_relu, done(half, K2))
                    for c in range(K2):
                        last = nc.tensor.matmul(mlp_ps[m % 2][:, 0:HALF], w2_sb[:, c, m * P:(m + 1) * P], h1[:, c, :],
                                                start=(c == 0), stop=(c == K2 - 1))
                    last.then_inc(h2_made, 1)
                pe.wait_ge(h2_relu, done(half, K3))
                pe.wait_ge(y_copied, free(half))
                for c in range(K3):
                    last = nc.tensor.matmul(y_ps[0:1, :], w3_sb[:, c:c + 1], h2[:, c, :],
                                            start=(c == 0), stop=(c == K3 - 1))
                last.then_inc(y_made, 1)

            for signal, count in ((summed, PRODS), (h1_made, K2), (h2_made, K3), (y_made, 1),
                                  *((n, SLOTS) for n in looked_up)):
                pe.sem_inc(signal, count)
            pe.wait_ge(low_made, KINDS)
            look_up(0, 0)
            pe.wait_ge(weights_loaded, 16 * 6)
            with pe.Fori(0, GROUPS - 1) as g:
                for s in range(SLOTS):
                    look_up(g + (s + 1) // SLOTS, (s + 1) % SLOTS)
                    sum_pairs(g, s)
                    if s % TILES == TILES - 1:
                        layers(2 * g + s // TILES)
            for s in range(SLOTS):
                if s + 1 < SLOTS:
                    look_up(GROUPS - 1, s + 1)
                sum_pairs(GROUPS - 1, s)
                if s % TILES == TILES - 1:
                    layers(2 * (GROUPS - 1) + s // TILES)


LOOK_UP = ((1000, 32, 2), (1250, 32, 2), (12500, 2, 10))


def plan(row_counts):
    kinds, order, column = [], [], 3
    for rows, most, outer in LOOK_UP:
        fields = [f for f, n in enumerate(row_counts) if n == rows][:most]
        partitions = next(p for p in range(P, 0, -1) if rows % (p * outer) == 0)
        kinds.append(Kind(str(rows), len(fields), len(order), partitions, outer, rows // (partitions * outer),
                          column))
        column += outer
        order += fields
    return kinds, order + [f for f in range(len(row_counts)) if f not in order]


def kernel(**inputs):
    import numpy as np
    import concourse.bacc as bacc
    from concourse.bass_utils import run_bass_kernel_spmd

    nc = bacc.Bacc("TRN2", target_bir_lowering=False, num_devices=1)
    arrays = {}

    def dram(name, a):
        a = np.ascontiguousarray(a)
        arrays[name] = a
        return nc.dram_tensor(name, a.shape, mybir.dt.from_np(a.dtype), kind="ExternalInput").ap()

    B, F = inputs["ids"].shape
    kinds, order = plan([inputs[f"tbl_{f}"].shape[0] for f in range(F)])
    looked = sum(k.fields for k in kinds)

    partition = np.arange(P)
    scale, shift = np.zeros(P), np.zeros(P)
    for k in kinds:
        fields = (partition % looked >= k.first) & (partition % looked < k.first + k.fields)
        scale[fields] = 1 / k.inner
        shift[fields] = -(k.inner - 1) / (2 * k.inner)
    columns = [np.ones(P), scale, shift]
    for k in kinds:
        columns += [-(partition * k.outer + a) for a in range(k.outer)]
    columns += [np.full(P, b) for b in range(max(k.inner for k in kinds))]
    consts = np.stack(columns, axis=1).astype(np.float32)

    blocks, pairs = pair_blocks(F)
    rows = []
    for half, _ in blocks:
        for lower in range(0, F, 2 * half):
            for b in range(lower + half, lower + 2 * half):
                for a in range(lower, lower + half):
                    i, j = sorted((order[a], order[b]))
                    rows.append(i * F - i * (i + 1) // 2 + j - i - 1)
    w1 = np.asarray(inputs["W_top1"])
    rows += range(pairs, w1.shape[0])

    def by_partition(v):
        return np.asarray(v).reshape(-1, P).T

    ids = np.asarray(inputs["ids"])[:, order]
    ids_by_half = ids[:, :looked].reshape(-1, P * TILES, looked).transpose(0, 2, 1).reshape(-1, P * TILES)
    looked_tables = [[dram(f"table_{f}", inputs[f"tbl_{f}"]) for f in order[k.first:k.first + k.fields]]
                     for k in kinds]
    gathered_tables = [dram(f"table_{f}", inputs[f"tbl_{f}"]) for f in order[looked:]]
    out = nc.dram_tensor("out", (B, 1), F32, kind="ExternalOutput").ap()
    dlrm_tower(nc, kinds, dram("dense", inputs["dense_ctx"]), dram("ids", ids), dram("ids_by_half", ids_by_half),
               looked_tables, gathered_tables, dram("consts", consts), dram("w1", w1[rows]),
               dram("b1", by_partition(inputs["b_top1"])), dram("w2", inputs["W_top2"]),
               dram("b2", by_partition(inputs["b_top2"])), dram("w3", by_partition(inputs["W_top3"])),
               dram("identity", np.eye(P, dtype=np.float32)), out)
    return run_bass_kernel_spmd(nc, [arrays], core_ids=[0]).results[0]["out"]
```

```python
from collections import namedtuple
from contextlib import ExitStack

import concourse.bass as bass
from concourse import mybir

P = 128
TILES = 2
SLOTS = 2 * TILES
PRODS = 2
ROUND = float(3 * 2 ** 22)

F32 = mybir.dt.float32
BF16 = mybir.dt.bfloat16
F16 = mybir.dt.float16
I32 = mybir.dt.int32
ALU = mybir.AluOpType
ACT = mybir.ActivationFunctionType
AX_X = mybir.AxisListType.X

Kind = namedtuple("Kind", "name fields first rows outer inner number")


def pair_blocks(fields):
    portions, column = [], 0

    def add(lower, upper, repeats, width, height):
        nonlocal column
        portions[-1].append((lower, upper, repeats, width, height, column))
        column += repeats * width * height

    half, quarter = fields // 2, fields // 4
    for first, size in ((0, half), (half, quarter), (half + quarter, quarter)):
        portions.append([])
        if first:
            add(0, first, 1, half, size)
        if first > half:
            add(half, first, 1, quarter, size)
        width = size // 2
        while width:
            repeats = size // (2 * width)
            if repeats < width:
                for k in range(repeats):
                    at = first + 2 * width * k
                    add(at, at + width, 1, width, width)
            else:
                for j in range(width):
                    add(first, first + width + j, repeats, width, 1)
            width //= 2
    return portions, column


def free(turn, signals=1):
    return signals * (turn + 1)


def done(turn, signals=1, buffers=1):
    return signals * (turn + 1 + buffers)


def dlrm_tower(nc, kinds, dense, ids, ids_by_half, looked_tables, gathered_tables, consts, w1, b1, w2, b2, w3,
               identity, out):
    B, F = ids.shape
    D = gathered_tables[0].shape[1]
    TERMS = D // 2
    KINDS = len(kinds)
    LOOKED = sum(k.fields for k in kinds)
    GATHERED = F - LOOKED
    N1, N2 = w1.shape[1], w2.shape[1]
    ND = dense.shape[1]
    HALF = P * TILES
    HALVES = B // HALF
    GROUPS = B // (P * SLOTS)
    K1, K2, K3 = w1.shape[0] // P, N1 // P, N2 // P
    portions, PAIRS = pair_blocks(F)
    ENDS = (F // 2, F // 2 + F // 4, F)
    COLUMNS = [blocks[0][-1] for blocks in portions] + [PAIRS]
    IOTA = consts.shape[1] - max(k.inner for k in kinds)
    assert PAIRS + ND == w1.shape[0] and kinds[-1].outer % 2 == 0

    with ExitStack() as ctx:
        def sb(name, shape, dt=F32):
            return ctx.enter_context(nc.sbuf_tensor(name, shape, dt))

        def psum(name, shape):
            return ctx.enter_context(nc.psum_tensor(name, shape, F32))

        def sem(name):
            return ctx.enter_context(nc.semaphore(name))

        def sems(name, n):
            return [sem(f"{name}{i}") for i in range(n)]

        idx = sb("idx", [P, SLOTS, GATHERED], I32)
        idx_looked = sb("idx_looked", [P, B // P, LOOKED], I32)
        emb = sb("emb", [P, SLOTS, F * D])
        dense_sb = sb("dense_sb", [P, B // P, ND])
        prod = sb("prod", [P, PRODS, D, PAIRS + ND])
        zT = sb("zT", [P, K1, HALF])
        h1 = sb("h1", [P, K2, HALF])
        h2 = sb("h2", [P, K3, HALF])
        y = sb("y", [1, B])
        w1_sb = sb("w1_sb", [P, K1, N1])
        w2_sb = sb("w2_sb", [P, K2, N2])
        w3_sb = sb("w3_sb", [P, K3])
        b1_sb = sb("b1_sb", [P, K2])
        b2_sb = sb("b2_sb", [P, K3])
        ident = sb("ident", [P, P])
        const = sb("const", [P, consts.shape[1]])
        rows_in = sb("rows_in", [HALVES * LOOKED, HALF], I32)
        scaled_rows = sb("scaled_rows", [HALVES * LOOKED, HALF])
        numbers = sb("numbers", [HALVES * LOOKED, HALF], F16)
        numbers_dram = nc.dram_tensor("numbers_dram", (HALVES * LOOKED, HALF), F16, kind="Internal").ap()
        wide = sb("wide", [P, 2, LOOKED, HALF], F16)
        dist = sb("dist", [P, 2, kinds[-1].fields, HALF], BF16)
        hot = [sb(f"hot_{k.name}", [P, 2, k.outer, k.fields, HALF], BF16) for k in kinds]
        parts = [sb(f"parts_{k.name}", [P, k.fields * k.outer, 3, k.inner * D], BF16) for k in kinds]
        mask = [sb(f"mask_{k.name}", [P, B // P, k.fields, k.inner]) for k in kinds]
        picked = [sb(f"picked_{k.name}", [P, k.fields * k.inner, D]) for k in kinds]
        block_of = sb("block_of", [P, B // P, LOOKED])
        within = sb("within", [P, B // P, LOOKED])
        prod_flat = prod[:, :, :, :].rearrange("p b d q -> p (b d q)")
        raw, at = [], 0
        for k in kinds:
            size = k.fields * k.outer * k.inner * D
            raw.append(prod_flat[0:k.rows, at:at + size].rearrange("p (a c) -> p a c", c=k.inner * D))
            at += size

        tables = []
        for n, k in enumerate(kinds):
            lot = k.fields if k.outer * k.inner < P // 2 else 1
            tables += [(n, slice(f * k.outer, (f + lot) * k.outer)) for f in range(0, k.fields, lot)]

        zT_ps = [psum(f"zT_ps{i}", [P, K1, P]) for i in range(2)]
        mlp_ps = [psum(f"mlp_ps{i}", [P, 512]) for i in range(2)]
        y_ps = psum("y_ps", [1, HALF])
        rows_ps = [psum(f"rows_ps_{k.name}", [P, k.fields * k.inner * D]) for k in kinds]

        weights_loaded = sem("weights_loaded")
        const_loaded = sem("const_loaded")
        ids_loaded = sem("ids_loaded")
        tables_loaded = sems("tables_loaded", len(tables))
        high_made = sem("high_made")
        rest_made = sem("rest_made")
        middle_made = sem("middle_made")
        low_made = sem("low_made")
        blocks_found = sem("blocks_found")
        within_found = sem("within_found")
        masks_made = sem("masks_made")
        rows_in_loaded = sem("rows_in_loaded")
        rows_scaled = sem("rows_scaled")
        numbers_made = sem("numbers_made")
        numbers_stored = sem("numbers_stored")
        wide_loaded = sems("wide_loaded", 2)
        dist_made = sem("dist_made")
        hot_made = sems("hot_made", KINDS)
        looked_up = sems("looked_up", KINDS)
        masked = sems("masked", KINDS)
        selected = sem("selected")
        idx_loaded = sems("idx_loaded", SLOTS)
        dense_loaded = sem("dense_loaded")
        gather_begun = sem("gather_begun")
        gathered = [sems(f"gathered{s}_", 3) for s in range(SLOTS)]
        multiplied = sems("multiplied", SLOTS)
        halved = sem("halved")
        summed = sem("summed")
        zT_copied = sem("zT_copied")
        h1_made = sem("h1_made")
        h1_relu = sem("h1_relu")
        h2_made = sem("h2_made")
        h2_relu = sem("h2_relu")
        y_made = sem("y_made")
        y_copied = sem("y_copied")
        y_stored = sem("y_stored")

        block = ctx.enter_context(nc.Block())

        def load_wide(queue, q, half):
            numbers_by_half = numbers_dram.rearrange("(h f) n -> h (f n)", f=LOOKED)
            queue.dma_start(wide[:, q, :, :].rearrange("p f n -> p (f n)"),
                            numbers_by_half[bass.ds(half, 1), :].to_broadcast([P, LOOKED * HALF])
                            ).then_inc(wide_loaded[q], 16)

        @block.sync
        def _(sp):
            def load_idx(s, row):
                sp.dma_start(idx[:, s, :], ids[bass.ds(row, P), LOOKED:]).then_inc(idx_loaded[s], 16)

            load_idx(0, 0)
            sp.dma_start(rows_in[:, :], ids_by_half).then_inc(rows_in_loaded, 16)
            sp.dma_start(const[:, :], consts).then_inc(const_loaded, 16)
            sp.dma_start(idx_looked[:, :, :], ids.rearrange("(t p) f -> p t f", p=P)[:, :, 0:LOOKED]
                         ).then_inc(ids_loaded, 16)
            for i, (n, lot) in enumerate(tables):
                k = kinds[n]
                for p in (slice(0, k.rows // 16 * 16), slice(k.rows // 16 * 16, k.rows)):
                    sp.dma_start(raw[n][p, lot, :], looked_tables[n][p, lot, :]).then_inc(tables_loaded[i], 16)
            for s in range(1, SLOTS):
                load_idx(s, s * P)
            sp.dma_start(dense_sb[:, :, :], dense.rearrange("(t p) n -> p t n", p=P)).then_inc(dense_loaded, 16)
            with sp.Fori(1, GROUPS) as g:
                for s in range(SLOTS):
                    sp.wait_ge(multiplied[s], free(g, 2))
                    load_idx(s, (g * SLOTS + s) * P)
                    if s % TILES == 0:
                        load_wide(sp, s // TILES, 2 * g + s // TILES)

        @block.gpsimd
        def _(pool):
            with pool.Fori(0, GROUPS) as g:
                for s in range(SLOTS):
                    pool.wait_ge(multiplied[s], free(g, 2))
                    pool.wait_ge(idx_loaded[s], 16 * (g + 1))
                    pool.sem_inc(gather_begun, 1)
                    for i in range(GATHERED):
                        f = LOOKED + i
                        portion = sum(f >= end for end in ENDS)
                        nc.gpsimd.indirect_dma_start(
                            emb[:, s, f * D:(f + 1) * D], None, gathered_tables[i],
                            bass.IndirectOffsetOnAxis(ap=idx[:, s, i:i + 1], axis=0)).then_inc(gathered[s][portion], 16)

        @block.scalar
        def _(act):
            def one_hot(g, q):
                n, half = KINDS - 1, 2 * g + q
                k = kinds[n]

                def distance(a):
                    act.wait_ge(hot_made[n], free(k.outer * half + a))
                    nc.scalar.activation(dist[0:k.rows, a % 2, :, :],
                                         wide[0:k.rows, q, k.first:k.first + k.fields, :], ACT.Abs,
                                         bias=const[0:k.rows, k.number + a:k.number + a + 1]).then_inc(dist_made, 1)

                act.wait_ge(wide_loaded[q], 16 * (g + 1))
                act.wait_ge(looked_up[n], free(half, TILES))
                distance(0)
                for a in range(k.outer):
                    if a + 1 < k.outer:
                        distance(a + 1)
                    act.wait_ge(dist_made, k.outer * (half - 2) + a + 1)
                    nc.scalar.activation(hot[n][0:k.rows, q, a, :, :], dist[0:k.rows, a % 2, :, :],
                                         ACT.Relu, bias=const[0:k.rows, 0:1], scale=-1.0).then_inc(hot_made[n], 1)

            def copy_sums(tile, s):
                act.wait_ge(summed, done(tile, 1, PRODS))
                nc.scalar.copy(zT[:, :, (s % TILES) * P:(s % TILES + 1) * P], zT_ps[s % 2][:, :, :]
                               ).then_inc(zT_copied, 1)

            def layers(turn, sample, cols):
                width = cols.stop - cols.start
                act.wait_ge(h2_made, free(turn, K3))
                for m in range(K2):
                    act.wait_ge(h1_made, free(turn, K2) + m + 1)
                    nc.scalar.activation(h1[:, m, cols], mlp_ps[m % 2][:, cols], ACT.Relu,
                                         bias=b1_sb[:, m:m + 1]).then_inc(h1_relu, 1)
                act.wait_ge(y_made, free(turn))
                for m in range(K3):
                    act.wait_ge(h2_made, free(turn, K3) + m + 1)
                    nc.scalar.activation(h2[:, m, cols], mlp_ps[m % 2][:, cols], ACT.Relu,
                                         bias=b2_sb[:, m:m + 1]).then_inc(h2_relu, 1)
                act.wait_ge(y_made, done(turn))
                nc.scalar.copy(y[:, bass.ds(sample, width)], y_ps[0:1, cols]).then_inc(y_copied, 1)
                act.wait_ge(y_copied, done(turn))
                act.dma_start(out[bass.ds(sample, width), :].rearrange("b o -> o b"),
                              y[:, bass.ds(sample, width)]).then_inc(y_stored, 16)

            def half_work(g, q, ahead):
                half = 2 * g + q
                act.wait_ge(h1_made, free(half, K2))
                copy_sums(TILES * half, 0)
                if ahead:
                    one_hot(g + 1, q)
                copy_sums(TILES * half + 1, 1)
                layers(half, half * HALF, slice(0, HALF))

            def middle(i):
                n, field = tables[i]
                act.wait_ge(rest_made, i + 1)
                nc.scalar.copy(parts[n][0:kinds[n].rows, field, 1, :], raw[n][:, field, :]).then_inc(middle_made, 1)

            for signal, count in ((zT_copied, 2), (h1_relu, K2), (h2_relu, K3), (y_copied, 1)):
                act.sem_inc(signal, count)
            act.wait_ge(numbers_made, 1)
            act.dma_start(numbers_dram, numbers[:, :]).then_inc(numbers_stored, 16)
            act.wait_ge(numbers_stored, 16)
            load_wide(act, 0, 0)
            load_wide(act, 1, 1)
            for tensor, source in ((ident[:, :], identity), (b1_sb[:, :], b1), (b2_sb[:, :], b2), (w3_sb[:, :], w3),
                                   (w1_sb[:, :, :], w1.rearrange("(c p) n -> p c n", p=P)),
                                   (w2_sb[:, :, :], w2.rearrange("(c p) n -> p c n", p=P))):
                act.dma_start(tensor, source).then_inc(weights_loaded, 16)
            for i, (n, field) in enumerate(tables):
                k = kinds[n]
                act.wait_ge(tables_loaded[i], 32)
                nc.scalar.copy(parts[n][0:k.rows, field, 0, :], raw[n][:, field, :]).then_inc(high_made, 1)
                if i:
                    middle(i - 1)
            middle(len(tables) - 1)
            act.wait_ge(weights_loaded, 16 * 6)
            with act.Fori(0, GROUPS - 1) as g:
                half_work(g, 0, True)
                half_work(g, 1, True)
            half_work(GROUPS - 1, 0, False)
            act.wait_ge(h1_made, free(HALVES - 1, K2))
            for i in range(TILES):
                copy_sums(TILES * (HALVES - 1) + i, i)
                layers(HALVES - 1 + i, (HALVES - 1) * HALF + i * P, slice(i * P, (i + 1) * P))
            act.wait_ge(y_stored, 16 * (HALVES - 1 + TILES))

        @block.vector
        def _(dve):
            def make_masks():
                for k in kinds:
                    f = slice(k.first, k.first + k.fields)
                    nc.vector.tensor_scalar(within[:, :, f], idx_looked[:, :, f], -(k.inner - 1) / 2, 1.0 / k.inner,
                                            ALU.add, ALU.mult).then_inc(blocks_found, 1)
                dve.wait_ge(blocks_found, KINDS)
                nc.vector.tensor_scalar(block_of[:, :, :], within[:, :, :], ROUND, ROUND,
                                        ALU.add, ALU.subtract).then_inc(blocks_found, 1)
                dve.wait_ge(blocks_found, KINDS + 1)
                for k in kinds:
                    f = slice(k.first, k.first + k.fields)
                    nc.vector.scalar_tensor_tensor(within[:, :, f], block_of[:, :, f], -float(k.inner),
                                                   idx_looked[:, :, f], ALU.mult, ALU.add).then_inc(within_found, 1)
                dve.wait_ge(within_found, KINDS)
                for n, k in enumerate(kinds):
                    shape = [P, B // P, k.fields, k.inner]
                    nc.vector.tensor_tensor(
                        mask[n][:, :, :, :],
                        within[:, :, k.first:k.first + k.fields].unsqueeze(3).to_broadcast(shape),
                        const[:, IOTA:IOTA + k.inner].unsqueeze(1).unsqueeze(1).to_broadcast(shape),
                        ALU.is_equal).then_inc(masks_made, 1)

            def number_blocks():
                c = const[0:HALVES * LOOKED, :]
                nc.vector.tensor_scalar(scaled_rows[:, :], rows_in[:, :], c[:, 1:2], c[:, 2:3],
                                        ALU.mult, ALU.add).then_inc(rows_scaled, 1)
                dve.wait_ge(rows_scaled, 1)
                nc.vector.tensor_scalar(numbers[:, :], scaled_rows[:, :], ROUND, ROUND,
                                        ALU.add, ALU.subtract).then_inc(numbers_made, 1)

            def split_tables():
                for i in range(len(tables) + 1):
                    if i < len(tables):
                        n, lot = tables[i]
                        dve.wait_ge(high_made, i + 1)
                        nc.vector.tensor_tensor(raw[n][:, lot, :], raw[n][:, lot, :],
                                                parts[n][0:kinds[n].rows, lot, 0, :],
                                                ALU.subtract).then_inc(rest_made, 1)
                    if i:
                        n, lot = tables[i - 1]
                        dve.wait_ge(middle_made, i)
                        nc.vector.tensor_tensor(parts[n][0:kinds[n].rows, lot, 2, :], raw[n][:, lot, :],
                                                parts[n][0:kinds[n].rows, lot, 1, :],
                                                ALU.subtract).then_inc(low_made, 1)

            def one_hot(g, q, some):
                dve.wait_ge(wide_loaded[q], 16 * (g + 1))
                for n, k in enumerate(some):
                    dve.wait_ge(looked_up[n], free(2 * g + q, TILES))
                    for a in range(k.outer):
                        nc.vector.tensor_scalar(hot[n][0:k.rows, q, a, :, :],
                                                wide[0:k.rows, q, k.first:k.first + k.fields, :],
                                                const[0:k.rows, k.number + a:k.number + a + 1], 0.0,
                                                ALU.add, ALU.is_equal).then_inc(hot_made[n], 1)

            def select(g, s):
                tile = g * SLOTS + s
                for n, k in enumerate(kinds):
                    dve.wait_ge(looked_up[n], done(tile, 1, SLOTS))
                    dve.wait_ge(selected, KINDS * tile + n + 1)
                    at_tile = mask[n][:, bass.ds(tile, 1), :, :].rearrange("p t f a -> p (t f a)")
                    nc.vector.tensor_tensor(
                        picked[n][:, :, :], rows_ps[n][:, :].rearrange("p (a d) -> p a d", d=D),
                        at_tile.unsqueeze(2).to_broadcast([P, k.fields * k.inner, D]),
                        ALU.mult).then_inc(masked[n], 1)
                dve.wait_ge(multiplied[s], free(g, 2))
                for n, k in enumerate(kinds):
                    dve.wait_ge(masked[n], done(tile))
                    nc.vector.reduce_sum(
                        emb[:, s, k.first * D:(k.first + k.fields) * D].rearrange("p (f d) -> p f d", d=D),
                        picked[n][:, :, :].rearrange("p (f a) d -> p f d a", a=k.inner),
                        AX_X).then_inc(selected, 1)

            def multiply(s, lower, upper, repeats, width, height, column):
                o = prod[:, s % PRODS, :, column:column + repeats * width * height]
                if repeats == 1:
                    shape = [P, height, width, D]
                    low = fields_of(s, lower, width).unsqueeze(1).to_broadcast(shape)
                    high = fields_of(s, upper, height).unsqueeze(2).to_broadcast(shape)
                    o = o.rearrange("p d (j i) -> p j i d", j=height)
                else:
                    span = 2 * width * repeats
                    first = lower // span * span
                    low = fields_of(s, first, span).rearrange("p (r i) d -> p r i d", r=repeats)[:, :, 0:width, :]
                    j = upper - first
                    high = fields_of(s, first, span).rearrange("p (r i) d -> p r i d", r=repeats)[:, :, j:j + 1, :]
                    high = high.to_broadcast([P, repeats, width, D])
                    o = o.rearrange("p d (r i) -> p r i d", r=repeats)
                return nc.vector.tensor_tensor(o, low, high, ALU.mult)

            def fields_of(s, first, count):
                return emb[:, s, first * D:(first + count) * D].rearrange("p (f d) -> p f d", d=D)

            def halve(s, begin, end):
                terms = prod[:, s % PRODS, :, begin:end]
                nc.vector.tensor_tensor(terms[:, 0:TERMS, :], terms[:, 0:TERMS, :], terms[:, TERMS:, :],
                                        ALU.add).then_inc(halved, 1)

            def pairs(g, s):
                tile = g * SLOTS + s
                dve.wait_ge(summed, free(tile))
                at_tile = dense_sb[:, bass.ds(tile, 1), :].rearrange("p t n -> p (t n)")
                nc.vector.tensor_copy(prod[:, s % PRODS, 0, PAIRS:], at_tile)
                dve.wait_ge(selected, done(tile, KINDS))
                begin = LOOKED
                for n, blocks in enumerate(portions):
                    dve.wait_ge(gathered[s][n], 16 * (ENDS[n] - begin) * (g + 1))
                    begin = ENDS[n]
                    for b in blocks:
                        last = multiply(s, *b)
                    if n:
                        last.then_inc(multiplied[s], 1)
                        dve.wait_ge(multiplied[s], free(g, 2) + n)
                        halve(s, COLUMNS[n] if n > 1 else 0, COLUMNS[n + 1])

            for signal, count in ((selected, KINDS), *((h, 2) for h in hot_made), *((m, 1) for m in masked), *((m, 2) for m in multiplied)):
                dve.sem_inc(signal, count)
            dve.wait_ge(const_loaded, 16)
            dve.wait_ge(rows_in_loaded, 16)
            number_blocks()
            dve.wait_ge(ids_loaded, 16)
            make_masks()
            split_tables()
            dve.wait_ge(dense_loaded, 16)
            dve.wait_ge(masks_made, KINDS)
            dve.wait_ge(low_made, len(tables))
            one_hot(0, 0, kinds)
            select(0, 0)
            one_hot(0, 1, kinds)
            with dve.Fori(0, GROUPS - 1) as g:
                for s in range(SLOTS):
                    pairs(g, s)
                    if s % TILES == TILES - 1:
                        one_hot(g + 1, s // TILES, kinds[:-1])
                    select(g + (s + 1) // SLOTS, (s + 1) % SLOTS)
            for s in range(SLOTS):
                pairs(GROUPS - 1, s)
                if s + 1 < SLOTS:
                    select(GROUPS - 1, s + 1)

        @block.tensor
        def _(pe):
            def look_up(g, s):
                tile = g * SLOTS + s
                half = 2 * g + s // TILES
                cols = slice((s % TILES) * P, (s % TILES + 1) * P)
                for n, k in enumerate(kinds):
                    pe.wait_ge(hot_made[n], k.outer * (half + 1) + 2)
                    pe.wait_ge(masked[n], free(tile))
                    for f in range(k.fields):
                        for a in range(k.outer):
                            for part in range(3):
                                last = nc.tensor.matmul(
                                    rows_ps[n][:, f * k.inner * D:(f + 1) * k.inner * D],
                                    hot[n][0:k.rows, s // TILES, a, f, cols],
                                    parts[n][0:k.rows, f * k.outer + a, part, :],
                                    start=(a == 0 and part == 0), stop=(a == k.outer - 1 and part == 2))
                    last.then_inc(looked_up[n], 1)

            def sum_pairs(g, s):
                tile = g * SLOTS + s
                pe.wait_ge(zT_copied, free(tile))
                for c in range(K1):
                    pe.wait_ge(halved, 2 * tile + (1 if (c + 1) * P <= COLUMNS[2] else 2))
                    for d in range(TERMS):
                        n = P if d == 0 else min(P, PAIRS - c * P)
                        last = nc.tensor.matmul(
                            zT_ps[s % 2][0:n, c, :], prod[:, s % PRODS, d, c * P:c * P + n], ident[:, :],
                            start=(d == 0), stop=(d == TERMS - 1), is_transpose=True)
                last.then_inc(summed, 1)

            def layers(turn, last_tile, cols):
                pe.wait_ge(zT_copied, done(last_tile, 1, 2))
                for m in range(K2):
                    if m >= 2:
                        pe.wait_ge(h1_relu, free(turn, K2) + m - 1)
                    else:
                        pe.wait_ge(h2_relu, free(turn, K3))
                    for c in range(K1):
                        last = nc.tensor.matmul(mlp_ps[m % 2][:, cols], w1_sb[:, c, m * P:(m + 1) * P],
                                                zT[:, c, cols], start=(c == 0), stop=(c == K1 - 1))
                    last.then_inc(h1_made, 1)
                for m in range(K3):
                    pe.wait_ge(h1_relu, done(turn, K2))
                    for c in range(K2):
                        last = nc.tensor.matmul(mlp_ps[m % 2][:, cols], w2_sb[:, c, m * P:(m + 1) * P],
                                                h1[:, c, cols], start=(c == 0), stop=(c == K2 - 1))
                    last.then_inc(h2_made, 1)
                pe.wait_ge(h2_relu, done(turn, K3))
                pe.wait_ge(y_copied, free(turn))
                for c in range(K3):
                    last = nc.tensor.matmul(y_ps[0:1, cols], w3_sb[:, c:c + 1], h2[:, c, cols],
                                            start=(c == 0), stop=(c == K3 - 1))
                last.then_inc(y_made, 1)

            for signal, count in ((summed, PRODS), (h1_made, K2), (h2_made, K3), (y_made, 1),
                                  *((n, SLOTS) for n in looked_up)):
                pe.sem_inc(signal, count)
            pe.wait_ge(low_made, len(tables))
            look_up(0, 0)
            look_up(0, 1)
            pe.wait_ge(weights_loaded, 16 * 6)
            with pe.Fori(0, GROUPS - 1) as g:
                for s in range(SLOTS):
                    sum_pairs(g, s)
                    look_up(g + (s + 2) // SLOTS, (s + 2) % SLOTS)
                    if s % TILES == TILES - 1:
                        layers(2 * g + s // TILES, g * SLOTS + s, slice(0, HALF))
            for s in range(SLOTS):
                sum_pairs(GROUPS - 1, s)
                if s + 2 < SLOTS:
                    look_up(GROUPS - 1, s + 2)
                if s == TILES - 1:
                    layers(HALVES - 2, TILES * (HALVES - 1) - 1, slice(0, HALF))
                if s >= TILES:
                    layers(HALVES - 1 + s - TILES, SLOTS * (GROUPS - 1) + s,
                           slice((s - TILES) * P, (s - TILES + 1) * P))


LOOK_UP = ((1000, 32, 2), (1250, 32, 2), (12500, 2, 10))


def plan(row_counts):
    kinds, order, column = [], [], 3
    for rows, most, outer in LOOK_UP:
        fields = [f for f, n in enumerate(row_counts) if n == rows][:most]
        partitions = next(p for p in range(P, 0, -1) if rows % (p * outer) == 0)
        kinds.append(Kind(str(rows), len(fields), len(order), partitions, outer, rows // (partitions * outer),
                          column))
        column += outer
        order += fields
    return kinds, order + [f for f in range(len(row_counts)) if f not in order]


def kernel(**inputs):
    import numpy as np
    import concourse.bacc as bacc
    from concourse.bass_utils import run_bass_kernel_spmd

    nc = bacc.Bacc("TRN2", target_bir_lowering=False, num_devices=1)
    arrays = {}

    def dram(name, a):
        a = np.ascontiguousarray(a)
        arrays[name] = a
        return nc.dram_tensor(name, a.shape, mybir.dt.from_np(a.dtype), kind="ExternalInput").ap()

    B, F = inputs["ids"].shape
    kinds, order = plan([inputs[f"tbl_{f}"].shape[0] for f in range(F)])
    looked = sum(k.fields for k in kinds)

    partition = np.arange(P)
    scale, shift = np.zeros(P), np.zeros(P)
    for k in kinds:
        fields = (partition % looked >= k.first) & (partition % looked < k.first + k.fields)
        scale[fields] = 1 / k.inner
        shift[fields] = -(k.inner - 1) / (2 * k.inner)
    columns = [np.ones(P), scale, shift]
    for k in kinds:
        columns += [-(partition * k.outer + a) for a in range(k.outer)]
    columns += [np.full(P, b) for b in range(max(k.inner for k in kinds))]
    consts = np.stack(columns, axis=1).astype(np.float32)

    portions, pairs = pair_blocks(F)
    rows = []
    for lower, upper, repeats, width, height, _ in (b for blocks in portions for b in blocks):
        for at in range(0, 2 * width * repeats, 2 * width):
            for b in range(upper + at, upper + at + height):
                for a in range(lower + at, lower + at + width):
                    i, j = sorted((order[a], order[b]))
                    rows.append(i * F - i * (i + 1) // 2 + j - i - 1)
    w1 = np.asarray(inputs["W_top1"])
    rows += range(pairs, w1.shape[0])

    def by_partition(v):
        return np.asarray(v).reshape(-1, P).T

    ids = np.asarray(inputs["ids"])[:, order]
    ids_by_half = ids[:, :looked].reshape(-1, P * TILES, looked).transpose(0, 2, 1).reshape(-1, P * TILES)
    looked_tables = [
        dram(f"tables_{k.name}", np.concatenate(
            [np.asarray(inputs[f"tbl_{f}"]).reshape(k.rows, k.outer, -1) for f in order[k.first:k.first + k.fields]],
            axis=1))
        for k in kinds]
    gathered_tables = [dram(f"table_{f}", inputs[f"tbl_{f}"]) for f in order[looked:]]
    out = nc.dram_tensor("out", (B, 1), F32, kind="ExternalOutput").ap()
    dlrm_tower(nc, kinds, dram("dense", inputs["dense_ctx"]), dram("ids", ids), dram("ids_by_half", ids_by_half),
               looked_tables, gathered_tables, dram("consts", consts), dram("w1", w1[rows]),
               dram("b1", by_partition(inputs["b_top1"])), dram("w2", inputs["W_top2"]),
               dram("b2", by_partition(inputs["b_top2"])), dram("w3", by_partition(inputs["W_top3"])),
               dram("identity", np.eye(P, dtype=np.float32)), out)
    return run_bass_kernel_spmd(nc, [arrays], core_ids=[0]).results[0]["out"]
```

```python
from collections import namedtuple
from contextlib import ExitStack

import concourse.bass as bass
from concourse import mybir

P = 128
TILES = 2
SLOTS = 2 * TILES
GATHER_ALSO = (3,)
PRODS = 2
ROUND = float(3 * 2 ** 22)

F32 = mybir.dt.float32
BF16 = mybir.dt.bfloat16
F16 = mybir.dt.float16
I32 = mybir.dt.int32
ALU = mybir.AluOpType
ACT = mybir.ActivationFunctionType
AX_X = mybir.AxisListType.X

Kind = namedtuple("Kind", "name fields first rows outer inner number")


def pair_blocks(fields, column):
    sizes = (fields // 2, fields // 4, fields // 8, fields // 8)
    portions, ends = [], []
    for size in sizes:
        first = sum(sizes[:len(portions)])
        blocks = [(0, first, 1, first, size)] if first else []
        width = size // 2
        while width:
            repeats = size // (2 * width)
            if repeats < width:
                for at in range(first, first + size, 2 * width):
                    blocks.append((at, at + width, 1, width, width))
            else:
                for j in range(width):
                    blocks.append((first, first + width + j, repeats, width, 1))
            width //= 2
        portions.append([])
        for lower, upper, repeats, width, height in blocks:
            portions[-1].append((lower, upper, repeats, width, height, column))
            column += repeats * width * height
        ends.append(first + size)
    return portions, ends, column


def free(turn, signals=1):
    return signals * (turn + 1)


def done(turn, signals=1, buffers=1):
    return signals * (turn + 1 + buffers)


def dlrm_tower(nc, kinds, dense, ids, ids_by_half, looked_tables, gathered_tables, consts, w1, b1, w2, b2, w3,
               identity, out):
    B, F = ids.shape
    D = gathered_tables[0].shape[1]
    TERMS = D // 2
    KINDS = len(kinds)
    LOOKED = sum(k.fields for k in kinds)
    N1, N2 = w1.shape[1], w2.shape[1]
    ND = dense.shape[1]
    HALF = P * TILES
    HALVES = B // HALF
    GROUPS = B // (P * SLOTS)
    K1, K2, K3 = w1.shape[0] // P, N1 // P, N2 // P
    portions, ENDS, WIDTH = pair_blocks(F, ND)
    COLUMNS = [blocks[0][-1] for blocks in portions] + [WIDTH]
    PARTS = len(portions) - 1
    LOTS = [[(first, end)] for first, end in zip([0] + ENDS[:-1], ENDS)]
    for n in (1, PARTS):
        first, end = LOTS[n][0]
        LOTS[n] = [(first, (first + end) // 2), ((first + end) // 2, end)]
    WHOLE = COLUMNS[-2] // P
    GATES = [next(n for n in range(1, PARTS + 1) if COLUMNS[n + 1] >= (c + 1) * P) for c in range(WIDTH // P)]
    IOTA = consts.shape[1] - max(k.inner for k in kinds)
    assert WIDTH == w1.shape[0] and K2 == 4 and kinds[-1].outer % 2 == 0

    with ExitStack() as ctx:
        def sb(name, shape, dt=F32):
            return ctx.enter_context(nc.sbuf_tensor(name, shape, dt))

        def psum(name, shape):
            return ctx.enter_context(nc.psum_tensor(name, shape, F32))

        def sem(name):
            return ctx.enter_context(nc.semaphore(name))

        def sems(name, n):
            return [sem(f"{name}{i}") for i in range(n)]

        idx = sb("idx", [P, SLOTS, F - LOOKED + 1], I32)
        idx_looked = sb("idx_looked", [P, B // P, LOOKED], I32)
        emb = sb("emb", [P, SLOTS, F * D])
        dense_sb = sb("dense_sb", [P, B // P, ND])
        prod = sb("prod", [P, D + TERMS, WIDTH])
        zT = sb("zT", [P, K1, HALF])
        h1 = sb("h1", [P, K2, HALF])
        h2 = sb("h2", [P, K3, HALF])
        y = sb("y", [P, B // P])
        w1_sb = sb("w1_sb", [P, K1, N1])
        w2_sb = sb("w2_sb", [P, K2, N2])
        w3_sb = sb("w3_sb", [P, K3])
        b1_sb = sb("b1_sb", [P, K2])
        b2_sb = sb("b2_sb", [P, K3])
        ident = sb("ident", [P, P])
        const = sb("const", [P, consts.shape[1]])
        rows_in = sb("rows_in", [HALVES * LOOKED, HALF], I32)
        scaled_rows = sb("scaled_rows", [HALVES * LOOKED, HALF])
        numbers = sb("numbers", [HALVES * LOOKED, HALF], F16)
        numbers_dram = nc.dram_tensor("numbers_dram", (HALVES * LOOKED, HALF), F16, kind="Internal").ap()
        wide = sb("wide", [P, 2, LOOKED * HALF], F16)
        dist = [sb(f"dist_{k.name}", [P, 2 if k is kinds[-1] else 1, k.fields * HALF], BF16) for k in kinds]
        hot = [sb(f"hot_{k.name}", [P, 2, k.outer, k.fields * HALF], BF16) for k in kinds]
        parts = [sb(f"parts_{k.name}", [P, k.fields * k.outer, 3, k.inner * D], BF16) for k in kinds]
        mask = [sb(f"mask_{k.name}", [P, B // P, k.fields, k.inner], BF16) for k in kinds]
        picked = [sb(f"picked_{k.name}", [P, k.fields * k.inner, D]) for k in kinds]
        block_of = sb("block_of", [P, B // P, LOOKED])
        within = sb("within", [P, B // P, LOOKED])
        prod_flat = prod[:, :, :].rearrange("p d q -> p (d q)")
        raw, at = [], 0
        for k in kinds:
            size = k.fields * k.outer * k.inner * D
            raw.append(prod_flat[0:k.rows, at:at + size].rearrange("p (a c) -> p a c", c=k.inner * D))
            at += size

        tables = []
        for n, k in enumerate(kinds):
            lot = k.fields if k.outer * k.inner < P // 2 else 1
            tables += [(n, slice(f * k.outer, (f + lot) * k.outer)) for f in range(0, k.fields, lot)]

        zT_ps = [psum(f"zT_ps{i}", [P, K1, P]) for i in range(2)]
        mlp_ps = [psum(f"mlp_ps{i}", [P, 512]) for i in range(2)]
        y_ps = psum("y_ps", [P, TILES])
        rows_ps = [psum(f"rows_ps_{k.name}", [P, k.fields * k.inner * D]) for k in kinds]
        last_ps = mlp_ps + rows_ps[0:2]

        weights_loaded = sem("weights_loaded")
        const_loaded = sem("const_loaded")
        ids_loaded = sem("ids_loaded")
        tables_loaded = sems("tables_loaded", len(tables))
        high_made = sem("high_made")
        rest_made = sem("rest_made")
        middle_made = sem("middle_made")
        low_made = sem("low_made")
        blocks_found = sem("blocks_found")
        within_found = sem("within_found")
        masks_made = sem("masks_made")
        zeros_made = sem("zeros_made")
        rows_in_loaded = sem("rows_in_loaded")
        rows_scaled = sem("rows_scaled")
        numbers_made = sem("numbers_made")
        numbers_stored = sem("numbers_stored")
        wide_loaded = sems("wide_loaded", 2)
        dist_made = sems("dist_made", KINDS)
        hot_made = sems("hot_made", KINDS)
        vector_hot_made = sem("vector_hot_made")
        looked_up = sems("looked_up", KINDS)
        masked = sems("masked", KINDS)
        selected = sem("selected")
        idx_loaded = sems("idx_loaded", SLOTS)
        dense_loaded = sem("dense_loaded")
        gather_begun = sem("gather_begun")
        gathered = [{lot: sem(f"gathered{s}_{lot[0]}") for lots in LOTS for lot in lots} for s in range(SLOTS)]
        multiplied = sems("multiplied", SLOTS)
        halved = sem("halved")
        summed = sem("summed")
        whole_summed = sem("whole_summed")
        whole_copied = sem("whole_copied")
        zT_copied = sem("zT_copied")
        h1_made = sem("h1_made")
        h1_relu = sem("h1_relu")
        h2_made = sem("h2_made")
        h2_relu = sem("h2_relu")
        y_made = sem("y_made")
        y_copied = sem("y_copied")
        y_stored = sem("y_stored")

        LAST = KINDS - 1
        BY_ACT = [k.outer - (n == LAST - 1) for n, k in enumerate(kinds)]
        STEPS = [(n, a, step) for n in range(LAST) for a in range(BY_ACT[n]) for step in range(2)]
        assert len(STEPS) <= K2 + K3

        block = ctx.enter_context(nc.Block())

        def columns_of(n, q):
            return kinds[n].fields * HALF - (P if n == LAST and TILES * q + 1 in GATHER_ALSO else 0)

        def gathered_from(s):
            return LOOKED - (s in GATHER_ALSO)

        def wide_of(n, q):
            k = kinds[n]
            return wide[0:k.rows, q, k.first * HALF:k.first * HALF + columns_of(n, q)]

        def hot_of(n, q, a):
            return hot[n][0:kinds[n].rows, q, a, 0:columns_of(n, q)]

        def dist_of(n, q, a):
            return dist[n][0:kinds[n].rows, a % 2 if n == LAST else 0, 0:columns_of(n, q)]

        def looked_in(n, s):
            return kinds[n].fields - (n == LAST and s in GATHER_ALSO)

        def tiles_of(cols):
            return range(cols.start // P, cols.stop // P)

        def terms(s):
            first = D * (s % PRODS)
            return slice(first, first + TERMS)

        def load_wide(sp, q, half):
            numbers_by_half = numbers_dram.rearrange("(h f) n -> h (f n)", f=LOOKED)
            sp.dma_start(wide[:, q, :], numbers_by_half[bass.ds(half, 1), :].to_broadcast([P, LOOKED * HALF])
                         ).then_inc(wide_loaded[q], 16)

        @block.sync
        def _(sp):
            def load_idx(s, row):
                sp.dma_start(idx[:, s, :], ids[bass.ds(row, P), LOOKED - 1:]).then_inc(idx_loaded[s], 16)

            load_idx(0, 0)
            sp.dma_start(rows_in[:, :], ids_by_half).then_inc(rows_in_loaded, 16)
            sp.dma_start(const[:, :], consts).then_inc(const_loaded, 16)
            sp.dma_start(idx_looked[:, :, :], ids.rearrange("(t p) f -> p t f", p=P)[:, :, 0:LOOKED]
                         ).then_inc(ids_loaded, 16)
            for i, (n, lot) in enumerate(tables):
                k = kinds[n]
                if i + 1 == len(tables):
                    sp.wait_ge(numbers_stored, 16)
                    load_wide(sp, 0, 0)
                for p in (slice(0, k.rows // 16 * 16), slice(k.rows // 16 * 16, k.rows)):
                    sp.dma_start(raw[n][p, lot, :], looked_tables[n][p, lot, :]).then_inc(tables_loaded[i], 16)
            load_wide(sp, 1, 1)
            for s in range(1, SLOTS):
                load_idx(s, s * P)
            sp.dma_start(dense_sb[:, :, :], dense.rearrange("(t p) n -> p t n", p=P)).then_inc(dense_loaded, 16)
            for tensor, source in ((ident[:, :], identity), (b1_sb[:, :], b1), (b2_sb[:, :], b2), (w3_sb[:, :], w3),
                                   (w1_sb[:, :, :], w1.rearrange("(c p) n -> p c n", p=P)),
                                   (w2_sb[:, :, :], w2.rearrange("(c p) n -> p c n", p=P))):
                sp.dma_start(tensor, source).then_inc(weights_loaded, 16)
            with sp.Fori(1, GROUPS) as g:
                for s in range(SLOTS):
                    sp.wait_ge(multiplied[s], free(g, PARTS))
                    load_idx(s, (g * SLOTS + s) * P)
                    if s % TILES == 0:
                        load_wide(sp, s // TILES, 2 * g + s // TILES)

        @block.gpsimd
        def _(pool):
            with pool.Fori(0, GROUPS) as g:
                for s in range(SLOTS):
                    pool.wait_ge(multiplied[s], free(g, PARTS))
                    pool.wait_ge(idx_loaded[s], 16 * (g + 1))
                    pool.sem_inc(gather_begun, 1)
                    for f in range(gathered_from(s), F):
                        i = f - (LOOKED - 1)
                        lot = next(lot for lots in LOTS for lot in lots if f < lot[1])
                        nc.gpsimd.indirect_dma_start(
                            emb[:, s, f * D:(f + 1) * D], None, gathered_tables[i],
                            bass.IndirectOffsetOnAxis(ap=idx[:, s, i:i + 1], axis=0)).then_inc(gathered[s][lot], 16)

        @block.scalar
        def _(act):
            def distance(n, g, q, a):
                k = kinds[n]
                act.wait_ge(hot_made[n], BY_ACT[n] * (2 * g + q) + a + (1 if n == LAST else 2))
                nc.scalar.activation(dist_of(n, q, a), wide_of(n, q), ACT.Abs,
                                     bias=const[0:k.rows, k.number + a:k.number + a + 1]).then_inc(dist_made[n], 1)

            def one_hot(n, g, q, a):
                k = kinds[n]
                act.wait_ge(dist_made[n], BY_ACT[n] * (2 * g + q) + a + 1)
                nc.scalar.activation(hot_of(n, q, a), dist_of(n, q, a), ACT.Relu,
                                     bias=const[0:k.rows, 0:1], scale=-1.0).then_inc(hot_made[n], 1)

            def last_one_hots(g, q):
                act.wait_ge(wide_loaded[q], 16 * (g + 1))
                act.wait_ge(looked_up[LAST], free(2 * g + q, TILES))
                distance(LAST, g, q, 0)
                for a in range(kinds[LAST].outer):
                    if a + 1 < kinds[LAST].outer:
                        distance(LAST, g, q, a + 1)
                    one_hot(LAST, g, q, a)

            def small_one_hots(gap, ahead):
                if ahead and gap < len(STEPS):
                    n, a, step = STEPS[gap]
                    (distance, one_hot)[step](n, *ahead, a)

            def copy_sums(tile, s):
                act.wait_ge(summed, done(tile, 1, PRODS))
                nc.scalar.copy(zT[:, :, (s % TILES) * P:(s % TILES + 1) * P], zT_ps[s % 2][:, :, :]
                               ).then_inc(zT_copied, 1)

            def layers(turn, tile, cols, ahead=None, banks=mlp_ps):
                act.wait_ge(h2_made, free(turn, K3))
                if ahead:
                    for n in range(LAST):
                        act.wait_ge(looked_up[n], free(2 * ahead[0] + ahead[1], TILES))
                for m in range(K2):
                    act.wait_ge(h1_made, free(turn, K2) + m + 1)
                    nc.scalar.activation(h1[:, m, cols], banks[m % len(banks)][:, cols], ACT.Relu,
                                         bias=b1_sb[:, m:m + 1]).then_inc(h1_relu, 1)
                    small_one_hots(m, ahead)
                act.wait_ge(y_made, free(turn))
                for m in range(K3):
                    act.wait_ge(h2_made, free(turn, K3) + m + 1)
                    nc.scalar.activation(h2[:, m, cols], mlp_ps[m % 2][:, cols], ACT.Relu,
                                         bias=b2_sb[:, m:m + 1]).then_inc(h2_relu, 1)
                    small_one_hots(K2 + m, ahead)
                act.wait_ge(y_made, done(turn))
                tiles = tiles_of(cols)
                nc.scalar.copy(y[:, bass.ds(tile, len(tiles))], y_ps[:, tiles.start:tiles.stop]).then_inc(y_copied, 1)

            def half_work(g, q):
                half = 2 * g + q
                act.wait_ge(h1_made, free(half, K2))
                copy_sums(TILES * half, 0)
                last_one_hots(g + 1, q)
                copy_sums(TILES * half + 1, 1)
                layers(half, TILES * half, slice(0, HALF), (g + 1, q))

            def middle(i):
                n, field = tables[i]
                act.wait_ge(rest_made, i + 1)
                nc.scalar.copy(parts[n][0:kinds[n].rows, field, 1, :], raw[n][:, field, :]).then_inc(middle_made, 1)

            for signal, count in ((zT_copied, 2), (h1_relu, K2), (h2_relu, K3), (y_copied, 1),
                                  (dist_made[LAST], BY_ACT[LAST]),
                                  *((dist_made[n], 2 * BY_ACT[n]) for n in range(LAST))):
                act.sem_inc(signal, count)
            act.wait_ge(numbers_made, 1)
            act.dma_start(numbers_dram, numbers[:, :]).then_inc(numbers_stored, 16)
            for i, (n, field) in enumerate(tables):
                k = kinds[n]
                act.wait_ge(tables_loaded[i], 32)
                nc.scalar.copy(parts[n][0:k.rows, field, 0, :], raw[n][:, field, :]).then_inc(high_made, 1)
                if i:
                    middle(i - 1)
            middle(len(tables) - 1)
            last_one_hots(0, 1)
            act.wait_ge(weights_loaded, 16 * 6)
            with act.Fori(0, GROUPS - 1) as g:
                half_work(g, 0)
                half_work(g, 1)
            for s in range(SLOTS):
                turn, tile, cols = HALVES - 2 + s, SLOTS * (GROUPS - 1) + s, slice(s % TILES * P, (s % TILES + 1) * P)
                act.wait_ge(h1_made, free(turn, K2))
                if s < SLOTS - 1:
                    copy_sums(tile, s)
                    layers(turn, tile, cols)
                else:
                    act.wait_ge(whole_summed, 1)
                    nc.scalar.copy(zT[:, 0:WHOLE, cols], zT_ps[s % 2][:, 0:WHOLE, :]).then_inc(whole_copied, 1)
                    act.wait_ge(summed, done(tile, 1, PRODS))
                    nc.scalar.copy(zT[:, WHOLE:, cols], zT_ps[s % 2][:, WHOLE:, :]).then_inc(zT_copied, 1)
                    layers(turn, tile, cols, banks=last_ps)
            act.wait_ge(y_copied, free(HALVES - 2 + SLOTS))
            act.dma_start(out, y[:, :]).then_inc(y_stored, 16)
            act.wait_ge(y_stored, 16)

        @block.vector
        def _(dve):
            def make_masks():
                for k in kinds:
                    f = slice(k.first, k.first + k.fields)
                    nc.vector.tensor_scalar(within[:, :, f], idx_looked[:, :, f], -(k.inner - 1) / 2, 1.0 / k.inner,
                                            ALU.add, ALU.mult).then_inc(blocks_found, 1)
                dve.wait_ge(blocks_found, KINDS)
                nc.vector.tensor_scalar(block_of[:, :, :], within[:, :, :], ROUND, ROUND,
                                        ALU.add, ALU.subtract).then_inc(blocks_found, 1)
                dve.wait_ge(blocks_found, KINDS + 1)
                for k in kinds:
                    f = slice(k.first, k.first + k.fields)
                    nc.vector.scalar_tensor_tensor(within[:, :, f], block_of[:, :, f], -float(k.inner),
                                                   idx_looked[:, :, f], ALU.mult, ALU.add).then_inc(within_found, 1)
                dve.wait_ge(within_found, KINDS)
                for n, k in enumerate(kinds):
                    shape = [P, B // P, k.fields, k.inner]
                    nc.vector.tensor_tensor(
                        mask[n][:, :, :, :],
                        within[:, :, k.first:k.first + k.fields].unsqueeze(3).to_broadcast(shape),
                        const[:, IOTA:IOTA + k.inner].unsqueeze(1).unsqueeze(1).to_broadcast(shape),
                        ALU.is_equal).then_inc(masks_made, 1)

            def number_blocks():
                c = const[0:HALVES * LOOKED, :]
                nc.vector.tensor_scalar(scaled_rows[:, :], rows_in[:, :], c[:, 1:2], c[:, 2:3],
                                        ALU.mult, ALU.add).then_inc(rows_scaled, 1)
                dve.wait_ge(rows_scaled, 1)
                nc.vector.tensor_scalar(numbers[:, :], scaled_rows[:, :], ROUND, ROUND,
                                        ALU.add, ALU.subtract).then_inc(numbers_made, 1)

            def split_tables():
                for i in range(len(tables) + 1):
                    if i < len(tables):
                        n, lot = tables[i]
                        if i + 1 == len(tables):
                            first_one_hots(0, range(KINDS))
                        dve.wait_ge(high_made, i + 1)
                        nc.vector.tensor_tensor(raw[n][:, lot, :], raw[n][:, lot, :],
                                                parts[n][0:kinds[n].rows, lot, 0, :],
                                                ALU.subtract).then_inc(rest_made, 1)
                    if i:
                        n, lot = tables[i - 1]
                        dve.wait_ge(middle_made, i)
                        nc.vector.tensor_tensor(parts[n][0:kinds[n].rows, lot, 2, :], raw[n][:, lot, :],
                                                parts[n][0:kinds[n].rows, lot, 1, :],
                                                ALU.subtract).then_inc(low_made, 1)

            def one_hot(n, q, a):
                k = kinds[n]
                nc.vector.tensor_scalar(hot_of(n, q, a), wide_of(n, q),
                                        const[0:k.rows, k.number + a:k.number + a + 1], 0.0, ALU.add, ALU.is_equal
                                        ).then_inc(hot_made[n] if a < BY_ACT[n] else vector_hot_made, 1)

            def first_one_hots(q, some):
                dve.wait_ge(wide_loaded[q], 16)
                for n in some:
                    for a in range(kinds[n].outer):
                        one_hot(n, q, a)

            def select(g, s):
                tile = g * SLOTS + s
                for n, k in enumerate(kinds):
                    count = looked_in(n, s) * k.inner
                    dve.wait_ge(looked_up[n], done(tile, 1, SLOTS))
                    dve.wait_ge(selected, KINDS * tile + n + 1)
                    at_tile = mask[n][:, bass.ds(tile, 1), 0:looked_in(n, s), :].rearrange("p t f a -> p (t f a)")
                    nc.vector.tensor_tensor(
                        picked[n][:, 0:count, :], rows_ps[n][:, 0:count * D].rearrange("p (a d) -> p a d", d=D),
                        at_tile.unsqueeze(2).to_broadcast([P, count, D]), ALU.mult).then_inc(masked[n], 1)
                dve.wait_ge(multiplied[s], free(g, PARTS))
                for n, k in enumerate(kinds):
                    dve.wait_ge(masked[n], done(tile))
                    nc.vector.reduce_sum(
                        fields_of(s, k.first, looked_in(n, s)),
                        picked[n][:, 0:looked_in(n, s) * k.inner, :].rearrange("p (f a) d -> p f d a", a=k.inner),
                        AX_X).then_inc(selected, 1)

            def multiply(s, lower, upper, repeats, width, height, column):
                first = TERMS * (s % PRODS)
                o = prod[:, first:first + D, column:column + repeats * width * height]
                if repeats == 1:
                    shape = [P, height, width, D]
                    low = fields_of(s, lower, width).unsqueeze(1).to_broadcast(shape)
                    high = fields_of(s, upper, height).unsqueeze(2).to_broadcast(shape)
                    o = o.rearrange("p d (j i) -> p j i d", j=height)
                else:
                    span = 2 * width * repeats
                    base = lower // span * span
                    low = fields_of(s, base, span).rearrange("p (r i) d -> p r i d", r=repeats)[:, :, 0:width, :]
                    j = upper - base
                    high = fields_of(s, base, span).rearrange("p (r i) d -> p r i d", r=repeats)[:, :, j:j + 1, :]
                    high = high.to_broadcast([P, repeats, width, D])
                    o = o.rearrange("p d (r i) -> p r i d", r=repeats)
                return nc.vector.tensor_tensor(o, low, high, ALU.mult)

            def fields_of(s, first, count):
                return emb[:, s, first * D:(first + count) * D].rearrange("p (f d) -> p f d", d=D)

            def halve(s, begin, end):
                stay = prod[:, terms(s), begin:end]
                nc.vector.tensor_tensor(stay, stay, prod[:, TERMS:2 * TERMS, begin:end], ALU.add).then_inc(halved, 1)

            def pairs(g, s, split=False):
                tile = g * SLOTS + s
                dve.wait_ge(summed, free(tile))
                at_tile = dense_sb[:, bass.ds(tile, 1), :].rearrange("p t n -> p (t n)")
                nc.vector.tensor_copy(prod[:, terms(s).start, 0:ND], at_tile)
                dve.wait_ge(halved, free(tile, PARTS))
                dve.wait_ge(selected, done(tile, KINDS))
                for n, blocks in enumerate(portions):
                    for i, (first, end) in enumerate(LOTS[n]):
                        dve.wait_ge(gathered[s][first, end], 16 * (end - max(first, gathered_from(s))) * (g + 1))
                        if split and len(LOTS[n]) > 1:
                            lower, upper, repeats, width, height, column = blocks[0]
                            multiply(s, lower, first, repeats, width, end - first, column + (first - upper) * width)
                    for b in blocks[1:] if split and len(LOTS[n]) > 1 else blocks:
                        last = multiply(s, *b)
                    if n:
                        last.then_inc(multiplied[s], 1)
                        dve.wait_ge(multiplied[s], free(g, PARTS) + n)
                        halve(s, COLUMNS[n if n > 1 else 0], COLUMNS[n + 1])

            for signal, count in ((selected, KINDS), (halved, PARTS), *((h, 2) for h in hot_made),
                                  *((m, 1) for m in masked), *((m, PARTS) for m in multiplied)):
                dve.sem_inc(signal, count)
            dve.wait_ge(const_loaded, 16)
            dve.wait_ge(rows_in_loaded, 16)
            number_blocks()
            dve.wait_ge(ids_loaded, 16)
            make_masks()
            dve.wait_ge(masks_made, KINDS)
            split_tables()
            dve.wait_ge(low_made, len(tables))
            first_one_hots(1, range(LAST))
            for buffer in range(PRODS):
                t = terms(buffer)
                nc.vector.memset(prod[:, t.start + 1:t.stop, 0:ND], 0.0).then_inc(zeros_made, 1)
            dve.wait_ge(zeros_made, PRODS)
            dve.wait_ge(dense_loaded, 16)
            select(0, 0)
            with dve.Fori(0, GROUPS - 1) as g:
                for s in range(SLOTS):
                    pairs(g, s)
                    if s % TILES == TILES - 1:
                        q = s // TILES
                        dve.wait_ge(wide_loaded[q], 16 * (g + 2))
                        dve.wait_ge(looked_up[LAST - 1], free(2 * (g + 1) + q, TILES))
                        one_hot(LAST - 1, q, BY_ACT[LAST - 1])
                    select(g + (s + 1) // SLOTS, (s + 1) % SLOTS)
            for s in range(SLOTS):
                pairs(GROUPS - 1, s, split=s == SLOTS - 1)
                if s + 1 < SLOTS:
                    select(GROUPS - 1, s + 1)

        @block.tensor
        def _(pe):
            def look_up(g, s, first=False):
                tile = g * SLOTS + s
                half = 2 * g + s // TILES
                for n, k in enumerate(kinds):
                    pe.wait_ge(hot_made[n], BY_ACT[n] * (half + 1) + 2)
                    if BY_ACT[n] < k.outer:
                        pe.wait_ge(vector_hot_made, half + 1)
                    pe.wait_ge(masked[n], free(tile))
                    for f in range(looked_in(n, s)):
                        if first:
                            lots = [i for i, (m, lot) in enumerate(tables) if m == n and lot.start <= f * k.outer]
                            pe.wait_ge(low_made, lots[-1] + 1)
                        for a in range(k.outer):
                            for part in range(3):
                                last = nc.tensor.matmul(
                                    rows_ps[n][:, f * k.inner * D:(f + 1) * k.inner * D],
                                    hot[n][0:k.rows, s // TILES, a, bass.ds(f * HALF + s % TILES * P, P)],
                                    parts[n][0:k.rows, f * k.outer + a, part, :],
                                    start=(a == 0 and part == 0), stop=(a == k.outer - 1 and part == 2))
                    last.then_inc(looked_up[n], 1)

            def sum_pairs(g, s, chunks):
                tile = g * SLOTS + s
                pe.wait_ge(zT_copied, free(tile))
                for c in chunks:
                    pe.wait_ge(halved, free(tile, PARTS) + GATES[c])
                    for d in range(TERMS):
                        last = nc.tensor.matmul(
                            zT_ps[s % 2][:, c, :], prod[:, terms(s).start + d, c * P:(c + 1) * P], ident[:, :],
                            start=(d == 0), stop=(d == TERMS - 1), is_transpose=True)
                return last

            def second_layer(turn, cols, own_banks=False):
                if not own_banks:
                    pe.wait_ge(h1_relu, free(turn, K2) + K2 - 1)
                for m in range(K3):
                    for c in range(K2):
                        if m == 0 and (own_banks or c == K2 - 1):
                            pe.wait_ge(h1_relu, free(turn, K2) + c + 1)
                        last = nc.tensor.matmul(mlp_ps[m % 2][:, cols], w2_sb[:, c, m * P:(m + 1) * P],
                                                h1[:, c, cols], start=(c == 0), stop=(c == K2 - 1))
                    last.then_inc(h2_made, 1)

            def output(turn, cols):
                pe.wait_ge(y_copied, free(turn))
                pe.wait_ge(h2_relu, done(turn, K3))
                for t in tiles_of(cols):
                    for c in range(K3):
                        last = nc.tensor.matmul(y_ps[:, t:t + 1], h2[:, c, t * P:(t + 1) * P], w3_sb[:, c:c + 1],
                                                start=(c == 0), stop=(c == K3 - 1))
                last.then_inc(y_made, 1)

            def two_layers(turn, last_tile, cols):
                pe.wait_ge(zT_copied, done(last_tile, 1, 2))
                for m in range(K2):
                    if m >= 2:
                        pe.wait_ge(h1_relu, free(turn, K2) + m - 1)
                    else:
                        pe.wait_ge(h2_relu, free(turn, K3))
                    for c in range(K1):
                        last = nc.tensor.matmul(mlp_ps[m % 2][:, cols], w1_sb[:, c, m * P:(m + 1) * P],
                                                zT[:, c, cols], start=(c == 0), stop=(c == K1 - 1))
                    last.then_inc(h1_made, 1)
                second_layer(turn, cols)

            def last_tile(turn, s):
                tile = SLOTS * (GROUPS - 1) + s
                cols = slice(s % TILES * P, (s % TILES + 1) * P)

                def first_layer(chunks, features=range(K2)):
                    for m in features:
                        for c in chunks:
                            last = nc.tensor.matmul(last_ps[m][:, cols], w1_sb[:, c, m * P:(m + 1) * P],
                                                    zT[:, c, cols], start=(c == 0), stop=(c == K1 - 1))
                        if K1 - 1 in chunks:
                            last.then_inc(h1_made, 1)

                pe.wait_ge(h2_relu, free(turn, K3))
                for n in range(K2 - 2):
                    pe.wait_ge(masked[n], done(tile))
                pe.wait_ge(whole_copied, 1)
                first_layer(range(WHOLE), range(K2 // 2))
                sum_pairs(GROUPS - 1, s, range(WHOLE, K1)).then_inc(summed, 1)
                first_layer(range(WHOLE), range(K2 // 2, K2))
                pe.wait_ge(zT_copied, done(tile, 1, 2))
                first_layer(range(WHOLE, K1))
                second_layer(turn, cols, own_banks=True)
                output(turn, cols)

            for signal, count in ((summed, PRODS), (h1_made, K2), (h2_made, K3), (y_made, 1),
                                  *((n, SLOTS) for n in looked_up)):
                pe.sem_inc(signal, count)
            look_up(0, 0, first=True)
            look_up(0, 1)
            pe.wait_ge(weights_loaded, 16 * 6)
            sum_pairs(0, 0, range(K1)).then_inc(summed, 1)
            with pe.Fori(0, GROUPS - 1) as g:
                for s in range(SLOTS):
                    look_up(g + (s + 2) // SLOTS, (s + 2) % SLOTS)
                    half = 2 * g + s // TILES
                    if s % TILES == TILES - 1:
                        two_layers(half, g * SLOTS + s, slice(0, HALF))
                    sum_pairs(g + (s + 1) // SLOTS, (s + 1) % SLOTS, range(K1)).then_inc(summed, 1)
                    if s % TILES == TILES - 1:
                        output(half, slice(0, HALF))
            for s in range(SLOTS - 1):
                if s + 2 < SLOTS:
                    look_up(GROUPS - 1, s + 2)
                turn, cols = HALVES - 2 + s, slice(s % TILES * P, (s % TILES + 1) * P)
                two_layers(turn, SLOTS * (GROUPS - 1) + s, cols)
                if s + 2 < SLOTS:
                    sum_pairs(GROUPS - 1, s + 1, range(K1)).then_inc(summed, 1)
                else:
                    sum_pairs(GROUPS - 1, s + 1, range(WHOLE)).then_inc(whole_summed, 1)
                output(turn, cols)
            last_tile(HALVES - 2 + SLOTS - 1, SLOTS - 1)


LOOK_UP = ((1000, 32, 2), (1250, 32, 2), (12500, 3, 10))


def plan(row_counts):
    kinds, order, column = [], [], 3
    for rows, most, outer in LOOK_UP:
        fields = [f for f, n in enumerate(row_counts) if n == rows][:most]
        partitions = next(p for p in range(P, 0, -1) if rows % (p * outer) == 0)
        kinds.append(Kind(str(rows), len(fields), len(order), partitions, outer, rows // (partitions * outer),
                          column))
        column += outer
        order += fields
    return kinds, order + [f for f in range(len(row_counts)) if f not in order]


def kernel(**inputs):
    import numpy as np
    import concourse.bacc as bacc
    from concourse.bass_utils import run_bass_kernel_spmd

    nc = bacc.Bacc("TRN2", target_bir_lowering=False, num_devices=1)
    arrays = {}

    def dram(name, a):
        a = np.ascontiguousarray(a)
        arrays[name] = a
        return nc.dram_tensor(name, a.shape, mybir.dt.from_np(a.dtype), kind="ExternalInput").ap()

    B, F = inputs["ids"].shape
    kinds, order = plan([inputs[f"tbl_{f}"].shape[0] for f in range(F)])
    looked = sum(k.fields for k in kinds)

    partition = np.arange(P)
    scale, shift = np.zeros(P), np.zeros(P)
    for k in kinds:
        fields = (partition % looked >= k.first) & (partition % looked < k.first + k.fields)
        scale[fields] = 1 / k.inner
        shift[fields] = -(k.inner - 1) / (2 * k.inner)
    columns = [np.ones(P), scale, shift]
    for k in kinds:
        columns += [-(partition * k.outer + a) for a in range(k.outer)]
    columns += [np.full(P, b) for b in range(max(k.inner for k in kinds))]
    consts = np.stack(columns, axis=1).astype(np.float32)

    w1 = np.asarray(inputs["W_top1"])
    nd = inputs["dense_ctx"].shape[1]
    rows = list(range(w1.shape[0] - nd, w1.shape[0]))
    portions, _, _ = pair_blocks(F, nd)
    for lower, upper, repeats, width, height, _ in (b for blocks in portions for b in blocks):
        for at in range(0, 2 * width * repeats, 2 * width):
            for b in range(upper + at, upper + at + height):
                for a in range(lower + at, lower + at + width):
                    i, j = sorted((order[a], order[b]))
                    rows.append(i * F - i * (i + 1) // 2 + j - i - 1)

    def by_partition(v):
        return np.asarray(v).reshape(-1, P).T

    ids = np.asarray(inputs["ids"])[:, order]
    ids_by_half = ids[:, :looked].reshape(-1, P * TILES, looked).transpose(0, 2, 1).reshape(-1, P * TILES)
    looked_tables = [
        dram(f"tables_{k.name}", np.concatenate(
            [np.asarray(inputs[f"tbl_{f}"]).reshape(k.rows, k.outer, -1) for f in order[k.first:k.first + k.fields]],
            axis=1))
        for k in kinds]
    gathered_tables = [dram(f"table_{f}", inputs[f"tbl_{f}"]) for f in order[looked - 1:]]
    out = nc.dram_tensor("out", (P, B // P), F32, kind="ExternalOutput").ap()
    dlrm_tower(nc, kinds, dram("dense", inputs["dense_ctx"]), dram("ids", ids), dram("ids_by_half", ids_by_half),
               looked_tables, gathered_tables, dram("consts", consts), dram("w1", w1[rows]),
               dram("b1", by_partition(inputs["b_top1"])), dram("w2", inputs["W_top2"]),
               dram("b2", by_partition(inputs["b_top2"])), dram("w3", by_partition(inputs["W_top3"])),
               dram("identity", np.eye(P, dtype=np.float32)), out)
    return run_bass_kernel_spmd(nc, [arrays], core_ids=[0]).results[0]["out"].T.reshape(B, 1)
```
